# Optimizing a Trainium2 kernel written in Bass

```python
import numpy as np
import jax
import jax.numpy as jnp

def _softmax(x, axis=-1):
    return jax.nn.softmax(x, axis=axis)

def _gelu(x):
    return jax.nn.gelu(x, approximate=True)

def _silu(x):
    return jax.nn.silu(x)

def _sigmoid(x):
    return jax.nn.sigmoid(x)

def _layernorm(x, axis=-1, eps=1e-05):
    m = jnp.mean(x, axis=axis, keepdims=True)
    v = jnp.var(x, axis=axis, keepdims=True)
    return (x - m) / jnp.sqrt(v + eps)

def _scatter_add(tgt, idx, src, axis=0):
    return tgt.at[idx].add(src)

def _segment_sum(src, seg, n):
    return jax.ops.segment_sum(src, seg, n)
kernel_name = 'mk_dlrm_tower_d1_rec_r8_d40110'

def setup_inputs(seed: int=0):
    np.random.seed(seed)
    _w = jnp.asarray

    def _rec_inputs():
        import jax
        import jax.numpy as jnp
        _tk = jax.random.key(seed)
        dense_ctx = jax.random.normal(jax.random.fold_in(_tk, 190), (1024, 16), jnp.float32)
        ids = jnp.stack([jax.random.randint(jax.random.fold_in(_tk, 200 + f), (1024,), 0, v, jnp.int32) for f, v in enumerate([12500, 1250, 125000, 1250, 1000, 12500, 12500, 125000, 1000, 12500, 1000, 125000, 1250, 1250, 1250, 1000, 12500, 1250, 12500, 125000, 12500, 1250, 125000, 1000, 1000, 1250, 1000, 125000, 125000, 1250, 1250, 1000, 125000, 125000, 1250, 1000, 1250, 1000, 125000])], axis=1)
        tbl_0 = 0.05 * jax.random.normal(jax.random.fold_in(_tk, 500 + 0), (12500, 16), jnp.float32)
        tbl_1 = 0.05 * jax.random.normal(jax.random.fold_in(_tk, 500 + 1), (1250, 16), jnp.float32)
        tbl_2 = 0.05 * jax.random.normal(jax.random.fold_in(_tk, 500 + 2), (125000, 16), jnp.float32)
        tbl_3 = 0.05 * jax.random.normal(jax.random.fold_in(_tk, 500 + 3), (1250, 16), jnp.float32)
        tbl_4 = 0.05 * jax.random.normal(jax.random.fold_in(_tk, 500 + 4), (1000, 16), jnp.float32)
        tbl_5 = 0.05 * jax.random.normal(jax.random.fold_in(_tk, 500 + 5), (12500, 16), jnp.float32)
        tbl_6 = 0.05 * jax.random.normal(jax.random.fold_in(_tk, 500 + 6), (12500, 16), jnp.float32)
        tbl_7 = 0.05 * jax.random.normal(jax.random.fold_in(_tk, 500 + 7), (125000, 16), jnp.float32)
        tbl_8 = 0.05 * jax.random.normal(jax.random.fold_in(_tk, 500 + 8), (1000, 16), jnp.float32)
        tbl_9 = 0.05 * jax.random.normal(jax.random.fold_in(_tk, 500 + 9), (12500, 16), jnp.float32)
        tbl_10 = 0.05 * jax.random.normal(jax.random.fold_in(_tk, 500 + 10), (1000, 16), jnp.float32)
        tbl_11 = 0.05 * jax.random.normal(jax.random.fold_in(_tk, 500 + 11), (125000, 16), jnp.float32)
        tbl_12 = 0.05 * jax.random.normal(jax.random.fold_in(_tk, 500 + 12), (1250, 16), jnp.float32)
        tbl_13 = 0.05 * jax.random.normal(jax.random.fold_in(_tk, 500 + 13), (1250, 16), jnp.float32)
        tbl_14 = 0.05 * jax.random.normal(jax.random.fold_in(_tk, 500 + 14), (1250, 16), jnp.float32)
        tbl_15 = 0.05 * jax.random.normal(jax.random.fold_in(_tk, 500 + 15), (1000, 16), jnp.float32)
        tbl_16 = 0.05 * jax.random.normal(jax.random.fold_in(_tk, 500 + 16), (12500, 16), jnp.float32)
        tbl_17 = 0.05 * jax.random.normal(jax.random.fold_in(_tk, 500 + 17), (1250, 16), jnp.float32)
        tbl_18 = 0.05 * jax.random.normal(jax.random.fold_in(_tk, 500 + 18), (12500, 16), jnp.float32)
        tbl_19 = 0.05 * jax.random.normal(jax.random.fold_in(_tk, 500 + 19), (125000, 16), jnp.float32)
        tbl_20 = 0.05 * jax.random.normal(jax.random.fold_in(_tk, 500 + 20), (12500, 16), jnp.float32)
        tbl_21 = 0.05 * jax.random.normal(jax.random.fold_in(_tk, 500 + 21), (1250, 16), jnp.float32)
        tbl_22 = 0.05 * jax.random.normal(jax.random.fold_in(_tk, 500 + 22), (125000, 16), jnp.float32)
        tbl_23 = 0.05 * jax.random.normal(jax.random.fold_in(_tk, 500 + 23), (1000, 16), jnp.float32)
        tbl_24 = 0.05 * jax.random.normal(jax.random.fold_in(_tk, 500 + 24), (1000, 16), jnp.float32)
        tbl_25 = 0.05 * jax.random.normal(jax.random.fold_in(_tk, 500 + 25), (1250, 16), jnp.float32)
        tbl_26 = 0.05 * jax.random.normal(jax.random.fold_in(_tk, 500 + 26), (1000, 16), jnp.float32)
        tbl_27 = 0.05 * jax.random.normal(jax.random.fold_in(_tk, 500 + 27), (125000, 16), jnp.float32)
        tbl_28 = 0.05 * jax.random.normal(jax.random.fold_in(_tk, 500 + 28), (125000, 16), jnp.float32)
        tbl_29 = 0.05 * jax.random.normal(jax.random.fold_in(_tk, 500 + 29), (1250, 16), jnp.float32)
        tbl_30 = 0.05 * jax.random.normal(jax.random.fold_in(_tk, 500 + 30), (1250, 16), jnp.float32)
        tbl_31 = 0.05 * jax.random.normal(jax.random.fold_in(_tk, 500 + 31), (1000, 16), jnp.float32)
        tbl_32 = 0.05 * jax.random.normal(jax.random.fold_in(_tk, 500 + 32), (125000, 16), jnp.float32)
        tbl_33 = 0.05 * jax.random.normal(jax.random.fold_in(_tk, 500 + 33), (125000, 16), jnp.float32)
        tbl_34 = 0.05 * jax.random.normal(jax.random.fold_in(_tk, 500 + 34), (1250, 16), jnp.float32)
        tbl_35 = 0.05 * jax.random.normal(jax.random.fold_in(_tk, 500 + 35), (1000, 16), jnp.float32)
        tbl_36 = 0.05 * jax.random.normal(jax.random.fold_in(_tk, 500 + 36), (1250, 16), jnp.float32)
        tbl_37 = 0.05 * jax.random.normal(jax.random.fold_in(_tk, 500 + 37), (1000, 16), jnp.float32)
        tbl_38 = 0.05 * jax.random.normal(jax.random.fold_in(_tk, 500 + 38), (125000, 16), jnp.float32)
        _rk = jax.random.fold_in(_tk, 7)
        W_top1 = 0.05 * jax.random.normal(jax.random.fold_in(_tk, 801), (400, 512), jnp.float32)
        W_top2 = 0.0441942 * jax.random.normal(jax.random.fold_in(_tk, 802), (512, 256), jnp.float32)
        W_top3 = 0.0625 * jax.random.normal(jax.random.fold_in(_tk, 803), (256, 1), jnp.float32)
        b_top1 = jnp.zeros((512,), jnp.float32)
        b_top2 = jnp.zeros((256,), jnp.float32)
        return (dense_ctx, ids, tbl_0, tbl_1, tbl_2, tbl_3, tbl_4, tbl_5, tbl_6, tbl_7, tbl_8, tbl_9, tbl_10, tbl_11, tbl_12, tbl_13, tbl_14, tbl_15, tbl_16, tbl_17, tbl_18, tbl_19, tbl_20, tbl_21, tbl_22, tbl_23, tbl_24, tbl_25, tbl_26, tbl_27, tbl_28, tbl_29, tbl_30, tbl_31, tbl_32, tbl_33, tbl_34, tbl_35, tbl_36, tbl_37, tbl_38, W_top1, b_top1, W_top2, b_top2, W_top3)
    dense_ctx, ids, tbl_0, tbl_1, tbl_2, tbl_3, tbl_4, tbl_5, tbl_6, tbl_7, tbl_8, tbl_9, tbl_10, tbl_11, tbl_12, tbl_13, tbl_14, tbl_15, tbl_16, tbl_17, tbl_18, tbl_19, tbl_20, tbl_21, tbl_22, tbl_23, tbl_24, tbl_25, tbl_26, tbl_27, tbl_28, tbl_29, tbl_30, tbl_31, tbl_32, tbl_33, tbl_34, tbl_35, tbl_36, tbl_37, tbl_38, W_top1, b_top1, W_top2, b_top2, W_top3 = _rec_inputs()

    def _L0_rec_setup():
        import jax, jax.numpy as jnp
        import numpy as np
        B, F0, D = (512, 39, 16)
        CIN = [128, 128, 128]

        def _cin_layer(X0, Xi, W, b):
            H = W.shape[0]
            F0_, Fi = (X0.shape[1], Xi.shape[1])
            Wr = W.reshape(H, F0_, Fi)
            return jnp.einsum('hjk,bjd,bkd->bhd', Wr, X0, Xi) + b[None, :, None]
        key = jax.random.key(seed)
        ks = jax.random.split(key, 4)
        x = jax.random.normal(ks[0], (B, F0, D), dtype=jnp.float32)
        fields = [F0] + CIN
        inp = {'embedded_features': x}
        for i in range(len(CIN)):
            cin = F0 * fields[i]
            cout = fields[i + 1]
            kw = jax.random.fold_in(ks[1], i)
            inp[f'W{i}'] = jax.random.normal(kw, (cout, cin), dtype=jnp.float32) / np.sqrt(cin)
            inp[f'b{i}'] = jnp.zeros((cout,), dtype=jnp.float32)
        return inp
    _L0_rec_all = _L0_rec_setup()
    _L0_rec_in = {k: v for k, v in _L0_rec_all.items() if k in ('W0', 'b0', 'W1', 'b1', 'W2', 'b2')}
    del _L0_rec_all
    return {'dense_ctx': dense_ctx, 'ids': ids, 'tbl_0': tbl_0, 'tbl_1': tbl_1, 'tbl_2': tbl_2, 'tbl_3': tbl_3, 'tbl_4': tbl_4, 'tbl_5': tbl_5, 'tbl_6': tbl_6, 'tbl_7': tbl_7, 'tbl_8': tbl_8, 'tbl_9': tbl_9, 'tbl_10': tbl_10, 'tbl_11': tbl_11, 'tbl_12': tbl_12, 'tbl_13': tbl_13, 'tbl_14': tbl_14, 'tbl_15': tbl_15, 'tbl_16': tbl_16, 'tbl_17': tbl_17, 'tbl_18': tbl_18, 'tbl_19': tbl_19, 'tbl_20': tbl_20, 'tbl_21': tbl_21, 'tbl_22': tbl_22, 'tbl_23': tbl_23, 'tbl_24': tbl_24, 'tbl_25': tbl_25, 'tbl_26': tbl_26, 'tbl_27': tbl_27, 'tbl_28': tbl_28, 'tbl_29': tbl_29, 'tbl_30': tbl_30, 'tbl_31': tbl_31, 'tbl_32': tbl_32, 'tbl_33': tbl_33, 'tbl_34': tbl_34, 'tbl_35': tbl_35, 'tbl_36': tbl_36, 'tbl_37': tbl_37, 'tbl_38': tbl_38, 'W_top1': W_top1, 'b_top1': b_top1, 'W_top2': W_top2, 'b_top2': b_top2, 'W_top3': W_top3, 'L0_rec_W0': _L0_rec_in['W0'], 'L0_rec_b0': _L0_rec_in['b0'], 'L0_rec_W1': _L0_rec_in['W1'], 'L0_rec_b1': _L0_rec_in['b1'], 'L0_rec_W2': _L0_rec_in['W2'], 'L0_rec_b2': _L0_rec_in['b2']}

def reference(dense_ctx, ids, tbl_0, tbl_1, tbl_2, tbl_3, tbl_4, tbl_5, tbl_6, tbl_7, tbl_8, tbl_9, tbl_10, tbl_11, tbl_12, tbl_13, tbl_14, tbl_15, tbl_16, tbl_17, tbl_18, tbl_19, tbl_20, tbl_21, tbl_22, tbl_23, tbl_24, tbl_25, tbl_26, tbl_27, tbl_28, tbl_29, tbl_30, tbl_31, tbl_32, tbl_33, tbl_34, tbl_35, tbl_36, tbl_37, tbl_38, W_top1, b_top1, W_top2, b_top2, W_top3, L0_rec_W0, L0_rec_b0, L0_rec_W1, L0_rec_b1, L0_rec_W2, L0_rec_b2):
    import jax
    import jax.numpy as jnp

    def _L0_rec_ref(embedded_features, W0, b0, W1, b1, W2, b2):
        import jax, jax.numpy as jnp
        import numpy as np
        B, F0, D = (512, 39, 16)
        CIN = [128, 128, 128]

        def _cin_layer(X0, Xi, W, b):
            H = W.shape[0]
            F0_, Fi = (X0.shape[1], Xi.shape[1])
            Wr = W.reshape(H, F0_, Fi)
            return jnp.einsum('hjk,bjd,bkd->bhd', Wr, X0, Xi) + b[None, :, None]
        X0 = embedded_features
        Ws = [(W0, b0), (W1, b1), (W2, b2)]
        Xi = X0
        res = []
        for W, b in Ws:
            Xi = _cin_layer(X0, Xi, W, b)
            res.append(Xi.sum(axis=2))
        return jnp.concatenate(res, axis=1)
    e = jnp.stack([tbl_0[ids[:, 0]], tbl_1[ids[:, 1]], tbl_2[ids[:, 2]], tbl_3[ids[:, 3]], tbl_4[ids[:, 4]], tbl_5[ids[:, 5]], tbl_6[ids[:, 6]], tbl_7[ids[:, 7]], tbl_8[ids[:, 8]], tbl_9[ids[:, 9]], tbl_10[ids[:, 10]], tbl_11[ids[:, 11]], tbl_12[ids[:, 12]], tbl_13[ids[:, 13]], tbl_14[ids[:, 14]], tbl_15[ids[:, 15]], tbl_16[ids[:, 16]], tbl_17[ids[:, 17]], tbl_18[ids[:, 18]], tbl_19[ids[:, 19]], tbl_20[ids[:, 20]], tbl_21[ids[:, 21]], tbl_22[ids[:, 22]], tbl_23[ids[:, 23]], tbl_24[ids[:, 24]], tbl_25[ids[:, 25]], tbl_26[ids[:, 26]], tbl_27[ids[:, 27]], tbl_28[ids[:, 28]], tbl_29[ids[:, 29]], tbl_30[ids[:, 30]], tbl_31[ids[:, 31]], tbl_32[ids[:, 32]], tbl_33[ids[:, 33]], tbl_34[ids[:, 34]], tbl_35[ids[:, 35]], tbl_36[ids[:, 36]], tbl_37[ids[:, 37]], tbl_38[ids[:, 38]]], axis=1)
    z = _L0_rec_ref(e, L0_rec_W0, L0_rec_b0, L0_rec_W1, L0_rec_b1, L0_rec_W2, L0_rec_b2)
    z = z.reshape(z.shape[0], -1)
    h = jnp.concatenate([z, dense_ctx], axis=1)
    h = jnp.maximum(h @ W_top1 + b_top1, 0.0)
    h = jnp.maximum(h @ W_top2 + b_top2, 0.0)
    y = h @ W_top3
    return y

_drawn_inputs = setup_inputs


def setup_inputs(seed=0):
    import zlib

    import numpy as np

    out = dict(_drawn_inputs(seed))
    spreads = {'b_top1': (0.0, 0.1),
     'b_top2': (0.0, 0.1),
     'L0_rec_b0': (0.0, 0.1),
     'L0_rec_b1': (0.0, 0.1),
     'L0_rec_b2': (0.0, 0.1)}
    factors = {'tbl_0': 8.0,
     'tbl_1': 5.781,
     'tbl_2': 5.233,
     'tbl_3': 7.053,
     'tbl_4': 8.0,
     'tbl_5': 8.0,
     'tbl_6': 8.0,
     'tbl_7': 6.676,
     'tbl_8': 8.0,
     'tbl_9': 8.0,
     'tbl_10': 8.0,
     'tbl_11': 6.458,
     'tbl_12': 8.0,
     'tbl_13': 8.0,
     'tbl_14': 4.189,
     'tbl_15': 5.382,
     'tbl_16': 8.0,
     'tbl_17': 8.0,
     'tbl_18': 8.0,
     'tbl_19': 5.76,
     'tbl_20': 7.325,
     'tbl_21': 8.0,
     'tbl_22': 8.0,
     'tbl_23': 8.0,
     'tbl_24': 8.0,
     'tbl_25': 7.262,
     'tbl_26': 5.671,
     'tbl_27': 8.0,
     'tbl_28': 8.0,
     'tbl_29': 8.0,
     'tbl_30': 6.581,
     'tbl_31': 6.036,
     'tbl_32': 8.0,
     'tbl_33': 7.099,
     'tbl_34': 8.0,
     'tbl_35': 7.533,
     'tbl_36': 8.0,
     'tbl_37': 6.571,
     'tbl_38': 8.0,
     'L0_rec_W0': 3.285}
    for name, (base, spread) in spreads.items():
        noise = np.random.default_rng([zlib.crc32(name.encode()), seed]).standard_normal(out[name].shape)
        drawn = base * np.exp(spread * noise) if base else spread * noise
        out[name] = jnp.asarray(drawn.astype(out[name].dtype))
    for name, factor in factors.items():
        out[name] = (out[name] * factor).astype(out[name].dtype)
    return out
```

```python
from contextlib import ExitStack

import concourse.bass as bass
from concourse import mybir

F32 = mybir.dt.float32
F32R = mybir.dt.float32r
I32 = mybir.dt.int32
ALU = mybir.AluOpType
ACT = mybir.ActivationFunctionType
AX = mybir.AxisListType

P = 128
BATCH, F, D, H = 1024, 39, 16, 128
TB = P // D
TILES = P // TB
GT = 4
GROUPS = TILES // GT
BLOCKS = BATCH // P
SHIFTS = 21
SPC = 3
CH = SHIFTS // SPC
KC = SPC * F
XW = F + SHIFTS - 1
XBW = XW + F + 1
FP = F + 1
JB = 4
FILLS = -(-F // JB)
YB = 4
ACT_FILLS = (0, 2, 4, 5, 7, 9)
DVE_FILLS = (1, 3, 6, 8)
NADD = 12
PART_A, PART_B = 2 * NADD, 2 * NADD + 1
A0, A1 = PART_B + 1, PART_B + 9
BIAS = F + 2
SLOTS = F + 3
L1D, L2D = 512, 256
HALF = 512
GATHER_TILES = 12


def slot(j):
    return j if j < PART_A else j + 2


def view(base, dims):
    return bass.AP(tensor=base.tensor, offset=base.offset, ap=[list(base.ap[0])] + dims)


def tr_index(g, k):
    return 9 * g + k + (4 if g == GROUPS - 1 else 0)


TR_ROWS = 9 * (GROUPS - 1)
TR_BLOCK = 9 * GROUPS + 4


def tr(B, n):
    return B * TR_BLOCK + (n + 1 + TR_BLOCK - TR_ROWS)


def tr_before(B, n, by):
    return B * TR_BLOCK + (n + 1 + TR_BLOCK - TR_ROWS - by)


def group(B, g):
    return B * GROUPS + (g + 2)


def pairs(B, g, u):
    return B * TILES + (GT * g + u + 5)


def tile(B, t):
    return B * TILES + (t + 2)


def fill(B, t, i):
    return B * (TILES * FILLS) + (t * FILLS + i + 1)


def used(B, t, fills, i):
    return B * (TILES * len(fills)) + ((t + 1) * len(fills) + fills.index(i) + 1)


def program(nc, a, out):
    with ExitStack() as ctx:
        def sb(name, shape, dt=F32):
            return ctx.enter_context(nc.sbuf_tensor(name, shape, dt))

        def psum(name, shape):
            return ctx.enter_context(nc.psum_tensor(name, shape, F32))

        def sem(name):
            return ctx.enter_context(nc.semaphore(name))

        ident = sb("ident", [P, P])
        mask = sb("mask", [P, TB])
        w0 = sb("w0", [KC, CH, H])
        w1hi = sb("w1hi", [P, F * H], F32R)
        w1lo = sb("w1lo", [P, F * H], F32R)
        w2 = sb("w2", [P, F, H])
        wt1 = sb("wt1", [P, 3, L1D])
        wt1d = sb("wt1d", [D, L1D])
        wt2 = sb("wt2", [P, L1D // P, L2D])
        wt3 = sb("wt3", [P, L2D // P])
        biases = sb("biases", [P, 2])
        biases_d = sb("biases_d", [P, 2])
        bt1 = sb("bt1", [P, L1D // P])
        bt2 = sb("bt2", [P, L2D // P])
        ids = sb("ids", [P, BLOCKS + 1, F], I32)
        ids_now = sb("ids_now", [P, F], I32)
        rows = sb("rows", [P, F, D])
        x0t = sb("x0t", [P, P, D])
        x0 = sb("x0", [P, 2, GT, XBW])
        pair = sb("pair", [P, 2, SHIFTS * F])
        pair_t = sb("pair_t", [KC, CH, GT * P])
        x1hi = sb("x1hi", [P, 2, GT * P], F32R)
        x1lo = sb("x1lo", [P, 2, GT * P], F32R)
        prod = sb("prod", [P, 2, SLOTS, H])
        x2 = sb("x2", [P, 2, H])
        diag = sb("diag", [P, 2, TB, FP])
        G = sb("G", [P, FP, P])
        z1 = sb("z1", [P, BATCH + GT * TB])
        z2 = sb("z2", [P, BATCH + P])
        z3 = sb("z3", [P, BATCH + P])
        dense = sb("dense", [D, BATCH])
        w1raw = prod[:, 0, 0:F, :].rearrange("p j h -> p (j h)")
        w0b = pair_t[:, :, 0:H]
        h1 = prod[:, 0, 0:L1D // P * BATCH // H, :].rearrange("p (m a) h -> p m (a h)", m=L1D // P)
        h2 = prod[:, 1, 0:L2D // P * BATCH // H, :].rearrange("p (m a) h -> p m (a h)", m=L2D // P)
        yrow = x0t[0:1, 0:BATCH // D, :].rearrange("p b d -> p (b d)")

        Y = psum("Y", [P, YB, 512])
        TR = psum("TR", [P, 2, 512])
        X1P = psum("X1P", [P, 512])
        GZ = psum("GZ", [P, 512])
        GP = GZ[:, 0:TB * FP]
        ZP = GZ[:, 384:512]

        ids_in = sem("ids_in")
        consts_in = sem("consts_in")
        w0_in = sem("w0_in")
        w1_in = sem("w1_in")
        rest_in = sem("rest_in")
        stored = sem("stored")
        gathered = sem("gathered")
        ids_copied = sem("ids_copied")
        w0_ready = sem("w0_ready")
        w1hi_ready = sem("w1hi_ready")
        w1lo_ready = sem("w1lo_ready")
        bias_ready = sem("bias_ready")
        ones_ready = sem("ones_ready")
        x0t_zeroed = sem("x0t_zeroed")
        G_zeroed = sem("G_zeroed")
        tr_full = sem("tr_full")
        tr_copied = sem("tr_copied")
        pairs_ready = sem("pairs_ready")
        x1_full = sem("x1_full")
        x1hi_ready = sem("x1hi_ready")
        x1lo_ready = sem("x1lo_ready")
        y_full = sem("y_full")
        y_act = sem("y_act")
        y_dve = sem("y_dve")
        added = sem("added")
        part_ready = sem("part_ready")
        x2_ready = sem("x2_ready")
        diag_ready = sem("diag_ready")
        g_full = sem("g_full")
        g_copied = sem("g_copied")
        z2_copied = sem("z2_copied")
        z3_full = sem("z3_full")
        z3_copied = sem("z3_copied")
        z1_done = sem("z1_done")
        h1_full = sem("h1_full")
        h1_ready = sem("h1_ready")
        h2_full = sem("h2_full")
        h2_ready = sem("h2_ready")
        y_row_full = sem("y_row_full")
        y_row = sem("y_row")

        block = ctx.enter_context(nc.Block())

        @block.sync
        def _(sp):
            sp.dma_start(ids[:, :, :], a["ids"]).then_inc(ids_in, 16)
            sp.dma_start(w1raw, a["w1"]).then_inc(w1_in, 16)
            sp.dma_start(ident[:, :], a["ident"]).then_inc(consts_in, 16)
            sp.dma_start(mask[:, :], a["mask"]).then_inc(consts_in, 16)
            sp.dma_start(biases[:, :], a["biases"]).then_inc(consts_in, 16)
            sp.dma_start(w0[:, :, :], a["w0a"]).then_inc(w0_in, 16)
            sp.dma_start(w0b, a["w0b"]).then_inc(w0_in, 16)
            for q in range(2):
                sp.dma_start(prod[:, q, BIAS, :], a["b1"].to_broadcast([P, H])).then_inc(rest_in, 16)
            sp.dma_start(w2[:, :, :], a["w2"]).then_inc(rest_in, 16)
            sp.dma_start(wt1[:, :, :], a["wt1"]).then_inc(rest_in, 16)
            sp.dma_start(wt1d[:, :], a["wt1d"]).then_inc(rest_in, 16)
            sp.dma_start(wt2[:, :, :], a["wt2"]).then_inc(rest_in, 16)
            sp.dma_start(wt3[:, :], a["wt3"]).then_inc(rest_in, 16)
            sp.dma_start(bt1[:, :], a["bt1"]).then_inc(rest_in, 16)
            sp.dma_start(bt2[:, :], a["bt2"]).then_inc(rest_in, 16)
            sp.dma_start(dense[:, :], a["dense"]).then_inc(rest_in, 16)
            sp.wait_ge(y_row, 2)
            sp.dma_start(out.rearrange("b o -> o b"), yrow).then_inc(stored, 16)
            sp.wait_ge(stored, 16)

        REST = 10 * 16

        @block.gpsimd
        def _(pool):
            def gather(f):
                pool.indirect_dma_start(
                    out=rows[:, f, :], out_offset=None, in_=a[f"tbl_{f}"],
                    in_offset=bass.IndirectOffsetOnAxis(ap=ids_now[:, f:f + 1], axis=0),
                ).then_inc(gathered, 16)

            def next_ids(B):
                pool.tensor_copy(ids_now[:, :], ids[:, bass.ds(B + 1, 1), :].rearrange("p o f -> p (o f)")
                                 ).then_inc(ids_copied, 1)

            pool.memset(x0t[:, :, :], 0.0).then_inc(x0t_zeroed, 1)
            pool.wait_ge(ids_in, 16)
            pool.tensor_copy(ids_now[:, :], ids[:, 0, :]).then_inc(ids_copied, 1)
            pool.wait_ge(ids_copied, 1)
            for f in range(F):
                gather(f)
            pool.memset(x0[:, :, :, XBW - 1:XBW], 1.0).then_inc(ones_ready, 1)
            pool.memset(prod[:, 1, 0:BIAS, :], 0.0).then_inc(added, 1)
            pool.memset(G[:, :, :], 0.0).then_inc(G_zeroed, 1)
            pool.memset(diag[:, 1, :, :], 0.0).then_inc(diag_ready, 1)
            pool.wait_ge(consts_in, 48)
            pool.wait_ge(ones_ready, 1)
            with pool.Fori(0, BLOCKS) as B:
                for t in range(TILES):
                    g, u, q = t // GT, t % GT, t % 2
                    if u == 0:
                        pool.wait_ge(tr_copied, tr(B, tr_index(g - 1, 0)) if g else tr(B - 1, tr_index(GROUPS - 1, 0)))
                    pool.wait_ge(g_full, B * TILES + t)
                    if t == 1:
                        pool.wait_ge(ids_copied, B + 2)
                    xs = x0[:, g % 2, u, XW:XBW]
                    pool.tensor_tensor(diag[:, q, :, :], view(xs, [[0, TB], [1, FP]]),
                                       view(mask[:, :], [[1, TB], [0, FP]]), ALU.mult).then_inc(diag_ready, 1)
                    if t == 0:
                        pool.wait_ge(gathered, (B + 1) * (16 * F))
                        pool.wait_ge(tr_full, tr(B - 1, TR_ROWS + 3))
                        next_ids(B)
                    if 0 < t < GATHER_TILES:
                        for f in range(F * (t - 1) // (GATHER_TILES - 1), F * t // (GATHER_TILES - 1)):
                            gather(f)
                    pool.wait_ge(y_act, used(B, t, ACT_FILLS, 5))
                    pool.wait_ge(y_dve, used(B, t, DVE_FILLS, 3))
                    pool.tensor_tensor(prod[:, q, NADD:2 * NADD, :], prod[:, q, 0:NADD, :],
                                       prod[:, q, NADD:2 * NADD, :], ALU.add).then_inc(added, 1)
            pool.wait_ge(gathered, (BLOCKS + 1) * (16 * F))

        @block.tensor
        def _(pe):
            def rows_ready(B, q):
                if q == 0:
                    pe.wait_ge(gathered, (B + 2) * (16 * F))
                if not (isinstance(B, int) and q < 2):
                    pe.wait_ge(tr_copied, tr_before(B, TR_ROWS + q, 2))

            def turn_rows(B, q):
                n = TR_ROWS + q
                for e in range(4):
                    mm = pe.transpose(TR[0:F, n % 2, P * e:P * e + P], rows[:, :, 4 * q + e], ident[:, :])
                mm.then_inc(tr_full, 1)

            def turn_x0(B, g):
                n = tr_index(g, 0)
                if g == GROUPS - 1:
                    pe.wait_ge(tr_copied, tr(B, TR_ROWS + 3))
                else:
                    pe.wait_ge(tr_copied, tr_before(B, n, 2))
                lo = (g + 1) % GROUPS * GT
                for u in range(GT):
                    mm = pe.transpose(TR[:, n % 2, P * u:P * u + P],
                                      x0t[:, (lo + u) * TB:(lo + u + 1) * TB, :].rearrange("f b d -> f (b d)"),
                                      ident[:, :])
                mm.then_inc(tr_full, 1)

            def turn_pairs(B, g, u):
                pe.wait_ge(pairs_ready, pairs(B, g, u))
                for half, chunks in enumerate((range(0, 4), range(4, CH))):
                    n = tr_index(g, 1 + 2 * u + half)
                    pe.wait_ge(tr_copied, tr_before(B, n, 2))
                    for c in chunks:
                        mm = pe.transpose(TR[0:KC, n % 2, P * (c - chunks[0]):P * (c - chunks[0]) + P],
                                          pair[:, u % 2, KC * c:KC * c + KC], ident[:, :])
                    mm.then_inc(tr_full, 1)

            def cin1(B, g, c):
                if c == 0:
                    pe.wait_ge(tr_copied, tr(B, tr_index(g, 2 * GT)))
                    pe.wait_ge(x1lo_ready, B * (2 * GROUPS) + (2 * (g + 1)))
                mm = pe.matmul(X1P[:, :], w0[:, c, :], pair_t[:, c, :], start=(c == 0), stop=(c == CH - 1))
                if c == CH - 1:
                    mm.then_inc(x1_full, 1)

            def cin2(B, t, i):
                g, u = t // GT, t % GT
                if u == 0 and i == 0:
                    pe.wait_ge(x1hi_ready, group(B, g - 1))
                    pe.wait_ge(x1lo_ready, B * (2 * GROUPS) + (2 * g + 1))
                tb, ib = (t, i - YB) if i >= YB else (t - 1, i - YB + FILLS)
                if ib in ACT_FILLS:
                    pe.wait_ge(y_act, used(B, tb, ACT_FILLS, ib))
                else:
                    pe.wait_ge(y_dve, used(B, tb, DVE_FILLS, ib))
                lo, hi = JB * H * i, min(JB * H * (i + 1), F * H)
                y = Y[:, (t * FILLS + i) % YB, 0:hi - lo]
                xh = x1hi[:, g % 2, P * u:P * u + P]
                xl = x1lo[:, g % 2, P * u:P * u + P]
                pe.matmul(y, xh, w1hi[:, lo:hi], start=True, stop=False)
                pe.matmul(y, xh, w1lo[:, lo:hi], start=False, stop=False)
                if t == (GROUPS - 1) * GT and i < 4:
                    rows_ready(B, i)
                pe.matmul(y, xl, w1hi[:, lo:hi], start=False, stop=True).then_inc(y_full, 1)

            def cin3_g(B, t):
                pe.wait_ge(x2_ready, tile(B, t))
                pe.wait_ge(diag_ready, tile(B, t))
                pe.wait_ge(g_copied, B * TILES + (t + 1))
                pe.matmul(GP, x2[:, t % 2, :], diag[:, t % 2, :, :].rearrange("p b j -> p (b j)"),
                          start=True, stop=True).then_inc(g_full, 1)

            def cin3_z(B, j):
                if j == 0:
                    pe.wait_ge(g_copied, B * TILES + 1)
                mm = pe.matmul(ZP, w2[:, j, :], G[:, j, :], start=(j == 0), stop=(j == F - 1))
                if j == F - 1:
                    mm.then_inc(z3_full, 1)

            pe.wait_ge(consts_in, 48)
            for q in range(4):
                rows_ready(-1, q)
                turn_rows(-1, q)
            turn_x0(-1, GROUPS - 1)
            for u in range(GT):
                turn_pairs(-1, GROUPS - 1, u)
            pe.wait_ge(w0_ready, 1)
            for c in range(CH):
                cin1(-1, GROUPS - 1, c)
            pe.wait_ge(w1hi_ready, 1)
            pe.wait_ge(w1lo_ready, 1)
            pe.wait_ge(rest_in, REST)
            pe.wait_ge(G_zeroed, 1)
            with pe.Fori(0, BLOCKS) as B:
                for t in range(TILES):
                    g, u = t // GT, t % GT
                    for i in range(FILLS):
                        cin2(B, t, i)
                        if u == 0:
                            if g == GROUPS - 1 and i < 4:
                                turn_rows(B, i)
                            if i == 6:
                                turn_x0(B, g)
                        if u == 1 and i == 6:
                            turn_pairs(B, g, 0)
                        if u == 2 and i in (0, 4, 8):
                            turn_pairs(B, g, 1 + i // 4)
                        if u == 3 and 1 <= i <= CH:
                            cin1(B, g, i - 1)
                        if t == 1 and i < 8:
                            for j in range(5 * i, min(5 * i + 5, F)):
                                cin3_z(B, j)
                        if i == 8:
                            if t == 1:
                                pe.wait_ge(z3_copied, B + 1)
                            cin3_g(B, t - 1)
            cin3_g(BLOCKS, -1)
            for j in range(F):
                cin3_z(BLOCKS, j)

            pe.wait_ge(z1_done, 1)
            for n in range(BATCH // HALF):
                s = HALF * n
                for m in range(L1D // P):
                    if n:
                        pe.wait_ge(h1_ready, L1D // P * (n - 1) + m + 1)
                    w = slice(P * m, P * m + P)
                    pe.matmul(Y[:, m, :], wt1d[:, w], dense[:, s:s + HALF], start=True, stop=False)
                    pe.matmul(Y[:, m, :], wt1[:, 0, w], z1[:, s:s + HALF], start=False, stop=False)
                    if n == 0 and m == 0:
                        pe.wait_ge(z2_copied, BLOCKS + 1)
                    pe.matmul(Y[:, m, :], wt1[:, 1, w], z2[:, P + s:P + s + HALF], start=False, stop=False)
                    if n == 0 and m == 0:
                        pe.wait_ge(z3_copied, BLOCKS + 1)
                    pe.matmul(Y[:, m, :], wt1[:, 2, w], z3[:, P + s:P + s + HALF], start=False,
                              stop=True).then_inc(h1_full, 1)
            for n in range(BATCH // HALF):
                s = HALF * n
                pe.wait_ge(h1_ready, L1D // P * (n + 1))
                for m in range(L2D // P):
                    if n:
                        pe.wait_ge(h2_ready, m + 1)
                    for k in range(L1D // P):
                        mm = pe.matmul(TR[:, m, :], wt2[:, k, P * m:P * m + P], h1[:, k, s:s + HALF],
                                       start=(k == 0), stop=(k == L1D // P - 1))
                    mm.then_inc(h2_full, 1)
            for n in range(BATCH // HALF):
                pe.wait_ge(h2_ready, L2D // P * (n + 1))
                for k in range(L2D // P):
                    mm = pe.matmul([X1P, GZ][n][0:1, :], wt3[:, k:k + 1], h2[:, k, HALF * n:HALF * (n + 1)],
                                   start=(k == 0), stop=(k == L2D // P - 1))
                mm.then_inc(y_row_full, 1)

        @block.scalar
        def _(act):
            def rows_out(B, q):
                n = TR_ROWS + q
                act.wait_ge(tr_full, tr(B, n))
                act.activation(x0t[0:F, :, 4 * q:4 * q + 4].rearrange("f b e -> f e b"),
                               TR[0:F, n % 2, :].rearrange("f (e b) -> f e b", e=4), ACT.Copy).then_inc(tr_copied, 1)

            def x0_out(B, g):
                n = tr_index(g, 0)
                act.wait_ge(tr_full, tr(B, n))
                if not isinstance(B, int):
                    act.wait_ge(diag_ready, tile(B, GT * g - 1))
                    act.wait_ge(y_dve, used(B, GT * g - 1, DVE_FILLS, DVE_FILLS[-1]))
                src = TR[:, n % 2, :].rearrange("p (u f) -> p u f", u=GT)[:, :, 0:F]
                dst = x0[:, (g + 1) % 2, :, :]
                act.activation(dst[:, :, 0:F], src, ACT.Copy)
                act.activation(dst[:, :, F:XW], src[:, :, 0:XW - F], ACT.Copy)
                act.activation(dst[:, :, XW:XW + F], src, ACT.Copy).then_inc(tr_copied, 1)

            def pairs_out(B, g, u):
                if u == 0 and not isinstance(B, int):
                    act.wait_ge(x1_full, B * GROUPS + (g + 1))
                for half, (c, d) in enumerate(((0, 4), (4, CH))):
                    n = tr_index(g, 1 + 2 * u + half)
                    act.wait_ge(tr_full, tr(B, n))
                    act.activation(pair_t[:, c:d, P * u:P * u + P],
                                   TR[0:KC, n % 2, 0:P * (d - c)].rearrange("p (c n) -> p c n", n=P),
                                   ACT.Copy).then_inc(tr_copied, 1)

            def x1_out(B, g):
                act.wait_ge(x1_full, group(B, g))
                act.activation(x1hi[:, (g + 1) % 2, :], X1P[:, :], ACT.Identity,
                               bias=biases[:, 0:1]).then_inc(x1hi_ready, 1)

            def multiply(B, t, i):
                g, u = t // GT, t % GT
                act.wait_ge(y_full, fill(B, t, i))
                for j in range(JB * i, min(JB * (i + 1), F)):
                    k = j - JB * i
                    ins = act.activation(prod[:, t % 2, slot(j), :], Y[:, (t * FILLS + i) % YB, H * k:H * k + H],
                                         ACT.Copy, scale=x0[:, g % 2, u, j:j + 1])
                ins.then_inc(y_act, 1)

            def g_out(B, t):
                act.wait_ge(g_full, tile(B, t))
                b = t % TILES * TB
                act.activation(G[:, :, b:b + TB].rearrange("k j b -> k b j"),
                               GP.rearrange("k (b j) -> k b j", b=TB), ACT.Copy).then_inc(g_copied, 1)

            def z2_out(B):
                act.wait_ge(g_copied, B * TILES + 1)
                act.activation(z2[:, bass.ds(B * P, P)], G[:, F, :], ACT.Copy).then_inc(z2_copied, 1)

            def z3_out(B):
                act.wait_ge(z3_full, B + 1)
                act.activation(z3[:, bass.ds(B * P, P)], ZP, ACT.Identity,
                               bias=biases_d[:, 1:2]).then_inc(z3_copied, 1)

            act.wait_ge(w1_in, 16)
            act.activation(w1hi[:, :], w1raw, ACT.Copy).then_inc(w1hi_ready, 1)
            act.wait_ge(consts_in, 48)
            act.activation(biases_d[:, :], biases[:, :], ACT.Copy, scale=float(D)).then_inc(bias_ready, 1)
            act.wait_ge(bias_ready, 1)
            act.wait_ge(x0t_zeroed, 1)
            for q in range(4):
                rows_out(-1, q)
            x0_out(-1, GROUPS - 1)
            act.wait_ge(w0_ready, 1)
            for u in range(GT):
                pairs_out(-1, GROUPS - 1, u)
            x1_out(-1, GROUPS - 1)
            act.wait_ge(w1lo_ready, 1)
            act.wait_ge(G_zeroed, 1)
            act.sem_inc(y_act, len(ACT_FILLS))
            with act.Fori(0, BLOCKS) as B:
                for t in range(TILES):
                    g, u = t // GT, t % GT
                    if u == 0:
                        act.wait_ge(tr_copied, tr(B, tr_index(g - 1, 0)) if g else tr(B - 1, tr_index(GROUPS - 1, 0)))
                    act.wait_ge(x2_ready, B * TILES + t)
                    multiply(B, t, 0)
                    if t == 1:
                        z2_out(B)
                    if t == (GROUPS - 1) * GT:
                        rows_out(B, 0)
                        rows_out(B, 1)
                    if u == 3:
                        pairs_out(B, g, 3)
                    multiply(B, t, 2)
                    if t == (GROUPS - 1) * GT:
                        rows_out(B, 2)
                        rows_out(B, 3)
                    if u == 2:
                        pairs_out(B, g, 1)
                    multiply(B, t, 4)
                    multiply(B, t, 5)
                    if u == 2:
                        pairs_out(B, g, 2)
                    multiply(B, t, 7)
                    if u == 0:
                        x0_out(B, g)
                    if u == 1:
                        pairs_out(B, g, 0)
                    if t == 1:
                        z3_out(B)
                    if u == 3:
                        x1_out(B, g)
                    multiply(B, t, 9)
                    g_out(B, t - 1)
            g_out(BLOCKS, -1)
            z2_out(BLOCKS)
            act.wait_ge(x1lo_ready, 2 * (BLOCKS * GROUPS + 1))
            act.activation(z1[:, 0:BATCH], z1[:, 0:BATCH], ACT.Identity, bias=biases_d[:, 0:1]).then_inc(z1_done, 1)
            z3_out(BLOCKS)
            act.wait_ge(rest_in, REST)
            for n in range(BATCH // HALF):
                for m in range(L1D // P):
                    act.wait_ge(h1_full, L1D // P * n + m + 1)
                    act.activation(h1[:, m, HALF * n:HALF * (n + 1)], Y[:, m, :], ACT.Relu,
                                   bias=bt1[:, m:m + 1]).then_inc(h1_ready, 1)
            for n in range(BATCH // HALF):
                for m in range(L2D // P):
                    act.wait_ge(h2_full, L2D // P * n + m + 1)
                    act.activation(h2[:, m, HALF * n:HALF * (n + 1)], TR[:, m, :], ACT.Relu,
                                   bias=bt2[:, m:m + 1]).then_inc(h2_ready, 1)
            for n in range(BATCH // HALF):
                act.wait_ge(y_row_full, n + 1)
                act.activation(yrow[:, HALF * n:HALF * (n + 1)], [X1P, GZ][n][0:1, :],
                               ACT.Copy).then_inc(y_row, 1)

        @block.vector
        def _(dve):
            def make_pairs(B, g, u):
                if u == 0:
                    dve.wait_ge(tr_copied, tr(B, tr_index(g, 0)))
                if u >= 2:
                    dve.wait_ge(tr_full, tr(B, tr_index(g, 2 * u - 2)))
                elif not isinstance(B, int):
                    dve.wait_ge(tr_full, tr(B, tr_index(g - 1, 2 * u + 6)) if g
                                else tr(B - 1, tr_index(GROUPS - 1, 2 * u + 6)))
                xs = x0[:, (g + 1) % 2, u, 0:XW]
                dve.tensor_tensor(view(pair[:, u % 2, :], [[F, SHIFTS], [1, F]]), view(xs, [[0, SHIFTS], [1, F]]),
                                  view(xs, [[1, SHIFTS], [1, F]]), ALU.mult).then_inc(pairs_ready, 1)

            def x1_low(B, g):
                dve.wait_ge(x1hi_ready, group(B, g))
                dve.scalar_tensor_tensor(out=x1lo[:, (g + 1) % 2, :], in0=X1P[:, :], scalar=biases[:, 0:1],
                                         in1=x1hi[:, (g + 1) % 2, :].bitcast(F32), op0=ALU.add,
                                         op1=ALU.subtract).then_inc(x1lo_ready, 1)

            def z1_sum(B, g):
                dve.tensor_reduce(z1[:, bass.ds(B * P + GT * TB * (g + 1), GT * TB)],
                                  X1P[:, :].rearrange("p (b d) -> p b d", d=D), AX.X, ALU.add
                                  ).then_inc(x1lo_ready, 1)

            def multiply(B, t, i):
                g, u = t // GT, t % GT
                dve.wait_ge(y_full, fill(B, t, i))
                xs = x0[:, g % 2, u, JB * i:JB * i + JB]
                dve.tensor_tensor(prod[:, t % 2, slot(JB * i):slot(JB * i) + JB, :],
                                  Y[:, (t * FILLS + i) % YB, :].rearrange("p (j h) -> p j h", h=H),
                                  view(xs, [[1, JB], [0, H]]), ALU.mult).then_inc(y_dve, 1)

            def add_up(dst, q, lo, hi, ready):
                dve.tensor_reduce(dst, prod[:, q, lo:hi, :].rearrange("p j h -> p h j"), AX.X, ALU.add
                                  ).then_inc(ready, 1)

            def part_b(B, t):
                dve.wait_ge(y_act, used(B, t, ACT_FILLS, 9))
                dve.wait_ge(y_dve, used(B, t, DVE_FILLS, 8))
                add_up(prod[:, t % 2, PART_B, :], t % 2, A1, SLOTS, part_ready)

            def part_a(B, t):
                dve.wait_ge(y_act, used(B, t, ACT_FILLS, 7))
                dve.wait_ge(y_dve, used(B, t, DVE_FILLS, 6))
                add_up(prod[:, t % 2, PART_A, :], t % 2, A0, A1, part_ready)

            def total(B, t):
                dve.wait_ge(part_ready, B * (2 * TILES) + (2 * t + 3))
                dve.wait_ge(added, tile(B, t))
                if not (isinstance(B, int) and B < 0):
                    dve.wait_ge(g_full, B * TILES + (t + 1))
                add_up(x2[:, t % 2, :], t % 2, NADD, PART_B + 1, x2_ready)

            dve.wait_ge(w1_in, 16)
            dve.wait_ge(w1hi_ready, 1)
            dve.tensor_tensor(w1lo[:, :], w1raw, w1hi[:, :].bitcast(F32), ALU.subtract).then_inc(w1lo_ready, 1)
            dve.wait_ge(w0_in, 32)
            dve.tensor_tensor(w0[:, :, :], w0[:, :, :], w0b, ALU.add).then_inc(w0_ready, 1)
            for u in range(GT):
                make_pairs(-1, GROUPS - 1, u)
            dve.wait_ge(consts_in, 48)
            x1_low(-1, GROUPS - 1)
            z1_sum(-1, GROUPS - 1)
            dve.wait_ge(rest_in, REST)
            dve.wait_ge(added, 1)
            dve.wait_ge(w1lo_ready, 1)
            dve.sem_inc(y_dve, len(DVE_FILLS))
            with dve.Fori(0, BLOCKS) as B:
                for t in range(TILES):
                    g, u = t // GT, t % GT
                    multiply(B, t, 1)
                    part_b(B, t - 1)
                    multiply(B, t, 3)
                    total(B, t - 1)
                    if u == 1:
                        make_pairs(B, g, 0)
                    if u == 2:
                        make_pairs(B, g, 2)
                    multiply(B, t, 6)
                    if u == 2:
                        make_pairs(B, g, 3)
                    multiply(B, t, 8)
                    if u == 1:
                        make_pairs(B, g, 1)
                    if u == 3:
                        x1_low(B, g)
                        z1_sum(B, g)
                    part_a(B, t)
            part_b(BLOCKS, -1)
            total(BLOCKS, -1)


def _layout(inputs):
    import numpy as np

    ids = np.asarray(inputs["ids"])
    blocks = ids.reshape(BLOCKS, P, F).transpose(1, 0, 2)
    w0 = np.asarray(inputs["L0_rec_W0"]).reshape(H, F, F)
    w0a = np.zeros((SHIFTS, F, H), w0.dtype)
    w0b = np.zeros((SHIFTS, F, H), w0.dtype)
    j = np.arange(F)
    for s in range(SHIFTS - 1):
        k = (j + s) % F
        w0a[s] = w0[:, j, k].T
        if s:
            w0b[s] = w0[:, k, j].T

    def chunks(w):
        return w.reshape(CH, KC, H).transpose(1, 0, 2)

    wt1 = np.asarray(inputs["W_top1"])
    arrays = {
        "ids": np.concatenate([blocks, blocks[:, :1]], axis=1),
        "ident": np.eye(P, dtype=np.float32),
        "mask": np.repeat(np.eye(TB, dtype=np.float32), D, axis=0),
        "biases": np.stack([inputs["L0_rec_b0"], inputs["L0_rec_b2"]], axis=1),
        "b1": np.asarray(inputs["L0_rec_b1"]).reshape(1, H),
        "w0a": chunks(w0a),
        "w0b": chunks(w0b),
        "w1": np.asarray(inputs["L0_rec_W1"]).reshape(H, F, H).transpose(2, 1, 0).reshape(P, F * H),
        "w2": np.asarray(inputs["L0_rec_W2"]).reshape(H, F, H).transpose(2, 1, 0),
        "wt1": wt1[:3 * P].reshape(3, P, L1D).transpose(1, 0, 2),
        "wt1d": wt1[3 * P:],
        "wt2": np.asarray(inputs["W_top2"]).reshape(L1D // P, P, L2D).transpose(1, 0, 2),
        "wt3": np.asarray(inputs["W_top3"]).reshape(L2D // P, P).T,
        "bt1": np.asarray(inputs["b_top1"]).reshape(L1D // P, P).T,
        "bt2": np.asarray(inputs["b_top2"]).reshape(L2D // P, P).T,
        "dense": np.asarray(inputs["dense_ctx"]).T,
    }
    for f in range(F):
        arrays[f"tbl_{f}"] = np.asarray(inputs[f"tbl_{f}"])
    return {n: np.ascontiguousarray(v) for n, v in arrays.items()}


def kernel(**inputs):
    import concourse.bacc as _bacc
    from concourse.bass_utils import run_bass_kernel_spmd as _run

    nc = _bacc.Bacc("TRN2", target_bir_lowering=False, num_devices=1)
    arrays = _layout(inputs)
    aps = {n: nc.dram_tensor(f"in_{n}", v.shape, mybir.dt.from_np(v.dtype), kind="ExternalInput").ap()
           for n, v in arrays.items()}
    y = nc.dram_tensor("y_out", (BATCH, 1), F32, kind="ExternalOutput").ap()
    program(nc, aps, y)
    r = _run(nc, [{f"in_{n}": v for n, v in arrays.items()}], core_ids=[0])
    return r.results[0]["y_out"]
```

```python
from contextlib import ExitStack

import concourse.bass as bass
from concourse import mybir

F32 = mybir.dt.float32
F32R = mybir.dt.float32r
I32 = mybir.dt.int32
ALU = mybir.AluOpType
ACT = mybir.ActivationFunctionType
AX = mybir.AxisListType

P = 128
BATCH, F, D, H = 1024, 39, 16, 128
TB = P // D
TILES = P // TB
GT = 4
GROUPS = TILES // GT
BLOCKS = BATCH // P
SHIFTS = 21
SPC = 3
CH = SHIFTS // SPC
KC = SPC * F
XW = F + SHIFTS - 1
XBW = XW + F + 1
FP = F + 1
JB = 4
FILLS = -(-F // JB)
YB = 4
ACT_FILLS = (0, 2, 4, 5, 7, 9)
DVE_FILLS = (1, 3, 6, 8)
NADD = 12
PART_A, PART_B = 2 * NADD, 2 * NADD + 1
A0, A1 = PART_B + 1, PART_B + 9
BIAS = F + 2
SLOTS = F + 3
L1D, L2D = 512, 256
HALF = 512
LEAD = 3
GATHER_TILES = 12


def slot(j):
    return j if j < PART_A else j + 2


def view(base, dims):
    return bass.AP(tensor=base.tensor, offset=base.offset, ap=[list(base.ap[0])] + dims)


TR_BLOCK = GROUPS + 2 * TILES + 4
T_ROWS = TILES - GT


def tr_rows(q):
    return 2 * T_ROWS + T_ROWS // GT + q


def tr_x0(t):
    return 2 * t + t // GT + (4 if t >= T_ROWS else 0)


def tr_pairs(t, half):
    return 2 * t + t // GT + 1 + half + (4 if t >= T_ROWS else 0)


def tr(B, n):
    return B * TR_BLOCK + (n + 1 + TR_BLOCK - tr_rows(0))


def tr_before(B, n, by):
    return B * TR_BLOCK + (n + 1 + TR_BLOCK - tr_rows(0) - by)


def last_x0(B, t):
    g = t // GT
    return tr(B, tr_x0(GT * (g - 1))) if g else tr(B - 1, tr_x0(T_ROWS))


def pairs(B, t):
    return B * TILES + (t + 1)


def x1(B, t):
    return B * TILES + (t + 1)


def tile(B, t):
    return B * TILES + (t + 2)


def fill(B, t, i):
    return B * (TILES * FILLS) + (t * FILLS + i + 1)


def used(B, t, fills, i):
    return B * (TILES * len(fills)) + ((t + 1) * len(fills) + fills.index(i) + 1)


def program(nc, a, out):
    with ExitStack() as ctx:
        def sb(name, shape, dt=F32):
            return ctx.enter_context(nc.sbuf_tensor(name, shape, dt))

        def psum(name, shape):
            return ctx.enter_context(nc.psum_tensor(name, shape, F32))

        def sem(name):
            return ctx.enter_context(nc.semaphore(name))

        ident = sb("ident", [P, P])
        mask = sb("mask", [P, TB])
        w0 = sb("w0", [KC, CH, H])
        w1hi = sb("w1hi", [P, F * H], F32R)
        w1lo = sb("w1lo", [P, F * H], F32R)
        w2 = sb("w2", [P, F, H])
        wt1 = sb("wt1", [P, 3, L1D])
        wt1d = sb("wt1d", [D, L1D])
        wt2 = sb("wt2", [P, L1D // P, L2D])
        wt3 = sb("wt3", [P, L2D // P])
        biases = sb("biases", [P, 2])
        biases_d = sb("biases_d", [P, 2])
        bt1 = sb("bt1", [P, L1D // P])
        bt2 = sb("bt2", [P, L2D // P])
        ids = sb("ids", [P, BLOCKS + 1, F], I32)
        ids_now = sb("ids_now", [P, F], I32)
        rows = sb("rows", [P, F, D])
        x0t = sb("x0t", [P, P, D])
        x0 = sb("x0", [P, 2, GT, XBW])
        pair = sb("pair", [P, 2, SHIFTS * F])
        pair_t = sb("pair_t", [KC, CH, P])
        x1hi = sb("x1hi", [P, 2, P], F32R)
        x1lo = sb("x1lo", [P, 2, P], F32R)
        prod = sb("prod", [P, 2, SLOTS, H])
        x2 = sb("x2", [P, 2, H])
        diag = sb("diag", [P, 2, TB, FP])
        G = sb("G", [P, FP, P])
        z1 = sb("z1", [P, BATCH + 2 * TB])
        z2 = sb("z2", [P, BATCH + P])
        z3 = sb("z3", [P, BATCH + P])
        dense = sb("dense", [D, BATCH])
        w1raw = prod[:, 0, 0:F, :].rearrange("p j h -> p (j h)")
        w0b = pair_t[:, :, :]
        h1 = prod[:, 0, 0:L1D // P * BATCH // H, :].rearrange("p (m a) h -> p m (a h)", m=L1D // P)
        h2 = prod[:, 1, 0:L2D // P * BATCH // H, :].rearrange("p (m a) h -> p m (a h)", m=L2D // P)
        yrow = x0t[0:1, 0:BATCH // D, :].rearrange("p b d -> p (b d)")

        Y = psum("Y", [P, YB, 512])
        TR = psum("TR", [P, 2, 512])
        X1P = psum("X1P", [P, 512])
        GZ = psum("GZ", [P, 512])
        GP = GZ[:, 0:TB * FP]
        ZP = GZ[:, 384:512]

        ids_in = sem("ids_in")
        consts_in = sem("consts_in")
        w0_in = sem("w0_in")
        w1_in = sem("w1_in")
        rest_in = sem("rest_in")
        stored = sem("stored")
        gathered = sem("gathered")
        ids_copied = sem("ids_copied")
        w0_ready = sem("w0_ready")
        w1hi_ready = sem("w1hi_ready")
        w1lo_ready = sem("w1lo_ready")
        bias_ready = sem("bias_ready")
        ones_ready = sem("ones_ready")
        x0t_zeroed = sem("x0t_zeroed")
        G_zeroed = sem("G_zeroed")
        tr_full = sem("tr_full")
        tr_copied = sem("tr_copied")
        pairs_ready = sem("pairs_ready")
        x1_full = sem("x1_full")
        x1hi_ready = sem("x1hi_ready")
        x1lo_ready = sem("x1lo_ready")
        y_full = sem("y_full")
        y_act = sem("y_act")
        y_dve = sem("y_dve")
        added = sem("added")
        part_ready = sem("part_ready")
        x2_ready = sem("x2_ready")
        diag_ready = sem("diag_ready")
        g_full = sem("g_full")
        g_copied = sem("g_copied")
        z2_copied = sem("z2_copied")
        z3_full = sem("z3_full")
        z3_copied = sem("z3_copied")
        z1_done = sem("z1_done")
        h1_full = sem("h1_full")
        h1_ready = sem("h1_ready")
        h2_full = sem("h2_full")
        h2_ready = sem("h2_ready")
        y_row_full = sem("y_row_full")
        y_row = sem("y_row")

        block = ctx.enter_context(nc.Block())

        @block.sync
        def _(sp):
            sp.dma_start(ids[:, :, :], a["ids"]).then_inc(ids_in, 16)
            sp.dma_start(w1raw, a["w1"]).then_inc(w1_in, 16)
            sp.dma_start(ident[:, :], a["ident"]).then_inc(consts_in, 16)
            sp.dma_start(mask[:, :], a["mask"]).then_inc(consts_in, 16)
            sp.dma_start(biases[:, :], a["biases"]).then_inc(consts_in, 16)
            sp.dma_start(w0[:, :, :], a["w0a"]).then_inc(w0_in, 16)
            sp.dma_start(w0b, a["w0b"]).then_inc(w0_in, 16)
            for q in range(2):
                sp.dma_start(prod[:, q, BIAS, :], a["b1"].to_broadcast([P, H])).then_inc(rest_in, 16)
            sp.dma_start(w2[:, :, :], a["w2"]).then_inc(rest_in, 16)
            sp.dma_start(wt1[:, :, :], a["wt1"]).then_inc(rest_in, 16)
            sp.dma_start(wt1d[:, :], a["wt1d"]).then_inc(rest_in, 16)
            sp.dma_start(wt2[:, :, :], a["wt2"]).then_inc(rest_in, 16)
            sp.dma_start(wt3[:, :], a["wt3"]).then_inc(rest_in, 16)
            sp.dma_start(bt1[:, :], a["bt1"]).then_inc(rest_in, 16)
            sp.dma_start(bt2[:, :], a["bt2"]).then_inc(rest_in, 16)
            sp.dma_start(dense[:, :], a["dense"]).then_inc(rest_in, 16)
            sp.wait_ge(y_row, 2)
            sp.dma_start(out.rearrange("b o -> o b"), yrow).then_inc(stored, 16)
            sp.wait_ge(stored, 16)

        REST = 10 * 16

        @block.gpsimd
        def _(pool):
            def gather(f):
                pool.indirect_dma_start(
                    out=rows[:, f, :], out_offset=None, in_=a[f"tbl_{f}"],
                    in_offset=bass.IndirectOffsetOnAxis(ap=ids_now[:, f:f + 1], axis=0),
                ).then_inc(gathered, 16)

            def next_ids(B):
                pool.tensor_copy(ids_now[:, :], ids[:, bass.ds(B + 1, 1), :].rearrange("p o f -> p (o f)")
                                 ).then_inc(ids_copied, 1)

            pool.memset(x0t[:, :, :], 0.0).then_inc(x0t_zeroed, 1)
            pool.wait_ge(ids_in, 16)
            pool.tensor_copy(ids_now[:, :], ids[:, 0, :]).then_inc(ids_copied, 1)
            pool.wait_ge(ids_copied, 1)
            for f in range(F):
                gather(f)
            pool.memset(x0[:, :, :, XBW - 1:XBW], 1.0).then_inc(ones_ready, 1)
            pool.memset(prod[:, 1, 0:BIAS, :], 0.0).then_inc(added, 1)
            pool.memset(G[:, :, :], 0.0).then_inc(G_zeroed, 1)
            pool.memset(diag[:, 1, :, :], 0.0).then_inc(diag_ready, 1)
            pool.wait_ge(consts_in, 48)
            pool.wait_ge(ones_ready, 1)
            with pool.Fori(0, BLOCKS) as B:
                for t in range(TILES):
                    g, u, q = t // GT, t % GT, t % 2
                    if u == 0:
                        pool.wait_ge(tr_copied, last_x0(B, t))
                    pool.wait_ge(g_full, B * TILES + t)
                    if t == 1:
                        pool.wait_ge(ids_copied, B + 2)
                    xs = x0[:, g % 2, u, XW:XBW]
                    pool.tensor_tensor(diag[:, q, :, :], view(xs, [[0, TB], [1, FP]]),
                                       view(mask[:, :], [[1, TB], [0, FP]]), ALU.mult).then_inc(diag_ready, 1)
                    if t == 0:
                        pool.wait_ge(gathered, (B + 1) * (16 * F))
                        pool.wait_ge(tr_full, tr(B - 1, tr_rows(3)))
                        next_ids(B)
                    if 0 < t < GATHER_TILES:
                        for f in range(F * (t - 1) // (GATHER_TILES - 1), F * t // (GATHER_TILES - 1)):
                            gather(f)
                    pool.wait_ge(y_act, used(B, t, ACT_FILLS, 5))
                    pool.wait_ge(y_dve, used(B, t, DVE_FILLS, 3))
                    pool.tensor_tensor(prod[:, q, NADD:2 * NADD, :], prod[:, q, 0:NADD, :],
                                       prod[:, q, NADD:2 * NADD, :], ALU.add).then_inc(added, 1)
            pool.wait_ge(gathered, (BLOCKS + 1) * (16 * F))

        @block.tensor
        def _(pe):
            def rows_ready(B, q):
                if q == 0:
                    pe.wait_ge(gathered, (B + 2) * (16 * F))
                if not (isinstance(B, int) and q < 2):
                    pe.wait_ge(tr_copied, tr_before(B, tr_rows(q), 2))

            def turn_rows(B, q):
                n = tr_rows(q)
                for e in range(4):
                    mm = pe.transpose(TR[0:F, n % 2, P * e:P * e + P], rows[:, :, 4 * q + e], ident[:, :])
                mm.then_inc(tr_full, 1)

            def turn_x0(B, t):
                n = tr_x0(t)
                if t == T_ROWS:
                    pe.wait_ge(tr_copied, tr(B, tr_rows(3)))
                else:
                    pe.wait_ge(tr_copied, tr_before(B, n, 2))
                lo = (t + GT) % TILES
                for u in range(GT):
                    mm = pe.transpose(TR[:, n % 2, P * u:P * u + P],
                                      x0t[:, (lo + u) * TB:(lo + u + 1) * TB, :].rearrange("f b d -> f (b d)"),
                                      ident[:, :])
                mm.then_inc(tr_full, 3 if isinstance(B, int) else 1)

            def turn_pairs(B, t):
                pe.wait_ge(pairs_ready, pairs(B, t + LEAD))
                for half, chunks in enumerate((range(0, 4), range(4, CH))):
                    n = tr_pairs(t, half)
                    pe.wait_ge(tr_copied, tr_before(B, n, 2))
                    for c in chunks:
                        mm = pe.transpose(TR[0:KC, n % 2, P * (c - chunks[0]):P * (c - chunks[0]) + P],
                                          pair[:, (t + LEAD) % 2, KC * c:KC * c + KC], ident[:, :])
                    mm.then_inc(tr_full, 1)

            def cin1(B, t, c):
                if c == 0:
                    pe.wait_ge(tr_copied, tr(B, tr_pairs(t - 1, 1)) if t else tr(B - 1, tr_pairs(TILES - 1, 1)))
                    pe.wait_ge(x1lo_ready, B * (2 * TILES) + (2 * (t + 2)))
                mm = pe.matmul(X1P[:, 0:P], w0[:, c, :], pair_t[:, c, :], start=(c == 0), stop=(c == CH - 1))
                if c == CH - 1:
                    mm.then_inc(x1_full, 1)

            def cin2(B, t, i):
                if i == 0:
                    pe.wait_ge(x1hi_ready, x1(B, t))
                    pe.wait_ge(x1lo_ready, B * (2 * TILES) + (2 * t + 1))
                tb, ib = (t, i - YB) if i >= YB else (t - 1, i - YB + FILLS)
                if ib in ACT_FILLS:
                    pe.wait_ge(y_act, used(B, tb, ACT_FILLS, ib))
                else:
                    pe.wait_ge(y_dve, used(B, tb, DVE_FILLS, ib))
                lo, hi = JB * H * i, min(JB * H * (i + 1), F * H)
                y = Y[:, (t * FILLS + i) % YB, 0:hi - lo]
                xh = x1hi[:, t % 2, :]
                xl = x1lo[:, t % 2, :]
                pe.matmul(y, xh, w1hi[:, lo:hi], start=True, stop=False)
                pe.matmul(y, xh, w1lo[:, lo:hi], start=False, stop=False)
                if t == T_ROWS and 1 <= i <= 4:
                    rows_ready(B, i - 1)
                pe.matmul(y, xl, w1hi[:, lo:hi], start=False, stop=True).then_inc(y_full, 1)

            def cin3_g(B, t):
                pe.wait_ge(x2_ready, tile(B, t))
                pe.wait_ge(diag_ready, tile(B, t))
                pe.wait_ge(g_copied, B * TILES + (t + 1))
                pe.matmul(GP, x2[:, t % 2, :], diag[:, t % 2, :, :].rearrange("p b j -> p (b j)"),
                          start=True, stop=True).then_inc(g_full, 1)

            def cin3_z(B, j):
                if j == 0:
                    pe.wait_ge(g_copied, B * TILES + 1)
                mm = pe.matmul(ZP, w2[:, j, :], G[:, j, :], start=(j == 0), stop=(j == F - 1))
                if j == F - 1:
                    mm.then_inc(z3_full, 1)

            pe.wait_ge(consts_in, 48)
            for q in range(4):
                rows_ready(-1, q)
                turn_rows(-1, q)
            turn_x0(-1, T_ROWS)
            turn_pairs(-1, TILES - 3)
            pe.wait_ge(w0_ready, 1)
            for t in range(TILES - 2, TILES):
                for c in range(CH):
                    cin1(-1, t, c)
                turn_pairs(-1, t)
            pe.wait_ge(w1hi_ready, 1)
            pe.wait_ge(w1lo_ready, 1)
            pe.wait_ge(rest_in, REST)
            pe.wait_ge(G_zeroed, 1)
            with pe.Fori(0, BLOCKS) as B:
                for t in range(TILES):
                    for i in range(FILLS):
                        cin2(B, t, i)
                        if t == T_ROWS and 1 <= i <= 4:
                            turn_rows(B, i - 1)
                        if t % GT == 0 and i == 6:
                            turn_x0(B, t)
                        if i >= 3:
                            cin1(B, t, i - 3)
                        if t == 1 and i < 8:
                            for j in range(5 * i, min(5 * i + 5, F)):
                                cin3_z(B, j)
                        if i == 8:
                            if t == 1:
                                pe.wait_ge(z3_copied, B + 1)
                            cin3_g(B, t - 1)
                    turn_pairs(B, t)
            cin3_g(BLOCKS, -1)
            for j in range(F):
                cin3_z(BLOCKS, j)

            pe.wait_ge(z1_done, 1)
            for n in range(BATCH // HALF):
                s = HALF * n
                for m in range(L1D // P):
                    if n:
                        pe.wait_ge(h1_ready, L1D // P * (n - 1) + m + 1)
                    w = slice(P * m, P * m + P)
                    pe.matmul(Y[:, m, :], wt1d[:, w], dense[:, s:s + HALF], start=True, stop=False)
                    pe.matmul(Y[:, m, :], wt1[:, 0, w], z1[:, s:s + HALF], start=False, stop=False)
                    if n == 0 and m == 0:
                        pe.wait_ge(z2_copied, BLOCKS + 1)
                    pe.matmul(Y[:, m, :], wt1[:, 1, w], z2[:, P + s:P + s + HALF], start=False, stop=False)
                    if n == 0 and m == 0:
                        pe.wait_ge(z3_copied, BLOCKS + 1)
                    pe.matmul(Y[:, m, :], wt1[:, 2, w], z3[:, P + s:P + s + HALF], start=False,
                              stop=True).then_inc(h1_full, 1)
            for n in range(BATCH // HALF):
                s = HALF * n
                pe.wait_ge(h1_ready, L1D // P * (n + 1))
                for m in range(L2D // P):
                    if n:
                        pe.wait_ge(h2_ready, m + 1)
                    for k in range(L1D // P):
                        mm = pe.matmul(TR[:, m, :], wt2[:, k, P * m:P * m + P], h1[:, k, s:s + HALF],
                                       start=(k == 0), stop=(k == L1D // P - 1))
                    mm.then_inc(h2_full, 1)
            for n in range(BATCH // HALF):
                pe.wait_ge(h2_ready, L2D // P * (n + 1))
                for k in range(L2D // P):
                    mm = pe.matmul([X1P, GZ][n][0:1, :], wt3[:, k:k + 1], h2[:, k, HALF * n:HALF * (n + 1)],
                                   start=(k == 0), stop=(k == L2D // P - 1))
                mm.then_inc(y_row_full, 1)

        @block.scalar
        def _(act):
            def rows_out(B, q):
                n = tr_rows(q)
                act.wait_ge(tr_full, tr(B, n))
                act.activation(x0t[0:F, :, 4 * q:4 * q + 4].rearrange("f b e -> f e b"),
                               TR[0:F, n % 2, :].rearrange("f (e b) -> f e b", e=4), ACT.Copy).then_inc(tr_copied, 1)

            def x0_out(B, t):
                n = tr_x0(t)
                act.wait_ge(tr_full, tr(B, n))
                if not isinstance(B, int):
                    act.wait_ge(diag_ready, tile(B, t - 1))
                    act.wait_ge(y_dve, used(B, t - 1, DVE_FILLS, DVE_FILLS[-1]))
                src = TR[:, n % 2, :].rearrange("p (u f) -> p u f", u=GT)[:, :, 0:F]
                dst = x0[:, (t // GT + 1) % 2, :, :]
                act.activation(dst[:, :, 0:F], src, ACT.Copy)
                act.activation(dst[:, :, F:XW], src[:, :, 0:XW - F], ACT.Copy)
                act.activation(dst[:, :, XW:XW + F], src, ACT.Copy).then_inc(
                    tr_copied, 3 if isinstance(B, int) else 1)

            def pairs_out(B, t):
                act.wait_ge(x1_full, B * TILES + (t + LEAD))
                for half, (c, d) in enumerate(((0, 4), (4, CH))):
                    n = tr_pairs(t, half)
                    act.wait_ge(tr_full, tr(B, n))
                    act.activation(pair_t[:, c:d, :],
                                   TR[0:KC, n % 2, 0:P * (d - c)].rearrange("p (c n) -> p c n", n=P),
                                   ACT.Copy).then_inc(tr_copied, 1)

            def x1_out(B, t):
                act.wait_ge(x1_full, x1(B, t))
                act.activation(x1hi[:, t % 2, :], X1P[:, 0:P], ACT.Identity,
                               bias=biases[:, 0:1]).then_inc(x1hi_ready, 1)

            def multiply(B, t, i):
                g, u = t // GT, t % GT
                act.wait_ge(y_full, fill(B, t, i))
                for j in range(JB * i, min(JB * (i + 1), F)):
                    k = j - JB * i
                    ins = act.activation(prod[:, t % 2, slot(j), :], Y[:, (t * FILLS + i) % YB, H * k:H * k + H],
                                         ACT.Copy, scale=x0[:, g % 2, u, j:j + 1])
                ins.then_inc(y_act, 1)

            def g_out(B, t):
                act.wait_ge(g_full, tile(B, t))
                b = t % TILES * TB
                act.activation(G[:, :, b:b + TB].rearrange("k j b -> k b j"),
                               GP.rearrange("k (b j) -> k b j", b=TB), ACT.Copy).then_inc(g_copied, 1)

            def z2_out(B):
                act.wait_ge(g_copied, B * TILES + 1)
                act.activation(z2[:, bass.ds(B * P, P)], G[:, F, :], ACT.Copy).then_inc(z2_copied, 1)

            def z3_out(B):
                act.wait_ge(z3_full, B + 1)
                act.activation(z3[:, bass.ds(B * P, P)], ZP, ACT.Identity,
                               bias=biases_d[:, 1:2]).then_inc(z3_copied, 1)

            act.wait_ge(w1_in, 16)
            act.activation(w1hi[:, :], w1raw, ACT.Copy).then_inc(w1hi_ready, 1)
            act.wait_ge(consts_in, 48)
            act.activation(biases_d[:, :], biases[:, :], ACT.Copy, scale=float(D)).then_inc(bias_ready, 1)
            act.wait_ge(bias_ready, 1)
            act.wait_ge(x0t_zeroed, 1)
            for q in range(4):
                rows_out(-1, q)
            x0_out(-1, T_ROWS)
            act.wait_ge(w0_ready, 1)
            pairs_out(-1, TILES - 3)
            x1_out(-1, TILES)
            pairs_out(-1, TILES - 2)
            act.wait_ge(w1lo_ready, 1)
            act.wait_ge(G_zeroed, 1)
            act.sem_inc(y_act, len(ACT_FILLS))
            with act.Fori(0, BLOCKS) as B:
                for t in range(TILES):
                    if t % GT == 0:
                        act.wait_ge(tr_copied, last_x0(B, t))
                    act.wait_ge(x2_ready, B * TILES + t)
                    multiply(B, t, 0)
                    x1_out(B, t + 1)
                    pairs_out(B - 1, TILES - 1) if t == 0 else pairs_out(B, t - 1)
                    if t == 1:
                        z2_out(B)
                    if t == T_ROWS:
                        rows_out(B, 0)
                    multiply(B, t, 2)
                    if t == T_ROWS:
                        rows_out(B, 1)
                        rows_out(B, 2)
                    multiply(B, t, 4)
                    if t == T_ROWS:
                        rows_out(B, 3)
                    multiply(B, t, 5)
                    multiply(B, t, 7)
                    if t % GT == 0:
                        x0_out(B, t)
                    if t == 1:
                        z3_out(B)
                    multiply(B, t, 9)
                    g_out(B, t - 1)
            g_out(BLOCKS, -1)
            z2_out(BLOCKS)
            act.wait_ge(x1lo_ready, 2 * (BLOCKS * TILES + 1))
            act.activation(z1[:, 0:BATCH], z1[:, 0:BATCH], ACT.Identity, bias=biases_d[:, 0:1]).then_inc(z1_done, 1)
            z3_out(BLOCKS)
            act.wait_ge(rest_in, REST)
            for n in range(BATCH // HALF):
                for m in range(L1D // P):
                    act.wait_ge(h1_full, L1D // P * n + m + 1)
                    act.activation(h1[:, m, HALF * n:HALF * (n + 1)], Y[:, m, :], ACT.Relu,
                                   bias=bt1[:, m:m + 1]).then_inc(h1_ready, 1)
            for n in range(BATCH // HALF):
                for m in range(L2D // P):
                    act.wait_ge(h2_full, L2D // P * n + m + 1)
                    act.activation(h2[:, m, HALF * n:HALF * (n + 1)], TR[:, m, :], ACT.Relu,
                                   bias=bt2[:, m:m + 1]).then_inc(h2_ready, 1)
            for n in range(BATCH // HALF):
                act.wait_ge(y_row_full, n + 1)
                act.activation(yrow[:, HALF * n:HALF * (n + 1)], [X1P, GZ][n][0:1, :],
                               ACT.Copy).then_inc(y_row, 1)

        @block.vector
        def _(dve):
            def make_pairs(B, t):
                if isinstance(B, int):
                    dve.wait_ge(tr_copied, tr(B, tr_x0(T_ROWS)))
                    if t == TILES + 2:
                        dve.wait_ge(tr_full, tr(B, tr_pairs(TILES - 3, 1)))
                else:
                    dve.wait_ge(tr_copied, last_x0(B, t) if t < TILES else tr(B, tr_x0(T_ROWS)))
                    p = t - 2 - LEAD
                    dve.wait_ge(tr_full, tr(B, tr_pairs(p, 1)) if p >= 0 else tr(B - 1, tr_pairs(p + TILES, 1)))
                xs = x0[:, t // GT % 2, t % GT, 0:XW]
                dve.tensor_tensor(view(pair[:, t % 2, :], [[F, SHIFTS], [1, F]]), view(xs, [[0, SHIFTS], [1, F]]),
                                  view(xs, [[1, SHIFTS], [1, F]]), ALU.mult).then_inc(pairs_ready, 1)

            def x1_low(B, t):
                dve.wait_ge(x1hi_ready, x1(B, t))
                dve.scalar_tensor_tensor(out=x1lo[:, t % 2, :], in0=X1P[:, 0:P], scalar=biases[:, 0:1],
                                         in1=x1hi[:, t % 2, :].bitcast(F32), op0=ALU.add,
                                         op1=ALU.subtract).then_inc(x1lo_ready, 1)

            def z1_sum(B, t):
                dve.tensor_reduce(z1[:, bass.ds(B * P + TB * t, TB)],
                                  X1P[:, 0:P].rearrange("p (b d) -> p b d", d=D), AX.X, ALU.add
                                  ).then_inc(x1lo_ready, 1)

            def multiply(B, t, i):
                g, u = t // GT, t % GT
                dve.wait_ge(y_full, fill(B, t, i))
                xs = x0[:, g % 2, u, JB * i:JB * i + JB]
                dve.tensor_tensor(prod[:, t % 2, slot(JB * i):slot(JB * i) + JB, :],
                                  Y[:, (t * FILLS + i) % YB, :].rearrange("p (j h) -> p j h", h=H),
                                  view(xs, [[1, JB], [0, H]]), ALU.mult).then_inc(y_dve, 1)

            def add_up(dst, q, lo, hi, ready):
                dve.tensor_reduce(dst, prod[:, q, lo:hi, :].rearrange("p j h -> p h j"), AX.X, ALU.add
                                  ).then_inc(ready, 1)

            def part_b(B, t):
                dve.wait_ge(y_act, used(B, t, ACT_FILLS, 9))
                dve.wait_ge(y_dve, used(B, t, DVE_FILLS, 8))
                add_up(prod[:, t % 2, PART_B, :], t % 2, A1, SLOTS, part_ready)

            def part_a(B, t):
                dve.wait_ge(y_act, used(B, t, ACT_FILLS, 7))
                dve.wait_ge(y_dve, used(B, t, DVE_FILLS, 6))
                add_up(prod[:, t % 2, PART_A, :], t % 2, A0, A1, part_ready)

            def total(B, t):
                dve.wait_ge(part_ready, B * (2 * TILES) + (2 * t + 3))
                dve.wait_ge(added, tile(B, t))
                if not (isinstance(B, int) and B < 0):
                    dve.wait_ge(g_full, B * TILES + (t + 1))
                add_up(x2[:, t % 2, :], t % 2, NADD, PART_B + 1, x2_ready)

            dve.wait_ge(w1_in, 16)
            dve.wait_ge(w1hi_ready, 1)
            dve.tensor_tensor(w1lo[:, :], w1raw, w1hi[:, :].bitcast(F32), ALU.subtract).then_inc(w1lo_ready, 1)
            dve.wait_ge(w0_in, 32)
            dve.tensor_tensor(w0[:, :, :], w0[:, :, :], w0b, ALU.add).then_inc(w0_ready, 1)
            for t in range(TILES, TILES + LEAD):
                make_pairs(-1, t)
            dve.wait_ge(consts_in, 48)
            x1_low(-1, TILES)
            z1_sum(-1, TILES)
            dve.wait_ge(rest_in, REST)
            dve.wait_ge(added, 1)
            dve.wait_ge(w1lo_ready, 1)
            dve.sem_inc(y_dve, len(DVE_FILLS))
            with dve.Fori(0, BLOCKS) as B:
                for t in range(TILES):
                    multiply(B, t, 1)
                    x1_low(B, t + 1)
                    z1_sum(B, t + 1)
                    part_b(B, t - 1)
                    multiply(B, t, 3)
                    total(B, t - 1)
                    multiply(B, t, 6)
                    make_pairs(B, t + LEAD)
                    multiply(B, t, 8)
                    part_a(B, t)
            part_b(BLOCKS, -1)
            total(BLOCKS, -1)


def _layout(inputs):
    import numpy as np

    ids = np.asarray(inputs["ids"])
    blocks = ids.reshape(BLOCKS, P, F).transpose(1, 0, 2)
    w0 = np.asarray(inputs["L0_rec_W0"]).reshape(H, F, F)
    w0a = np.zeros((SHIFTS, F, H), w0.dtype)
    w0b = np.zeros((SHIFTS, F, H), w0.dtype)
    j = np.arange(F)
    for s in range(SHIFTS - 1):
        k = (j + s) % F
        w0a[s] = w0[:, j, k].T
        if s:
            w0b[s] = w0[:, k, j].T

    def chunks(w):
        return w.reshape(CH, KC, H).transpose(1, 0, 2)

    wt1 = np.asarray(inputs["W_top1"])
    arrays = {
        "ids": np.concatenate([blocks, blocks[:, :1]], axis=1),
        "ident": np.eye(P, dtype=np.float32),
        "mask": np.repeat(np.eye(TB, dtype=np.float32), D, axis=0),
        "biases": np.stack([inputs["L0_rec_b0"], inputs["L0_rec_b2"]], axis=1),
        "b1": np.asarray(inputs["L0_rec_b1"]).reshape(1, H),
        "w0a": chunks(w0a),
        "w0b": chunks(w0b),
        "w1": np.asarray(inputs["L0_rec_W1"]).reshape(H, F, H).transpose(2, 1, 0).reshape(P, F * H),
        "w2": np.asarray(inputs["L0_rec_W2"]).reshape(H, F, H).transpose(2, 1, 0),
        "wt1": wt1[:3 * P].reshape(3, P, L1D).transpose(1, 0, 2),
        "wt1d": wt1[3 * P:],
        "wt2": np.asarray(inputs["W_top2"]).reshape(L1D // P, P, L2D).transpose(1, 0, 2),
        "wt3": np.asarray(inputs["W_top3"]).reshape(L2D // P, P).T,
        "bt1": np.asarray(inputs["b_top1"]).reshape(L1D // P, P).T,
        "bt2": np.asarray(inputs["b_top2"]).reshape(L2D // P, P).T,
        "dense": np.asarray(inputs["dense_ctx"]).T,
    }
    for f in range(F):
        arrays[f"tbl_{f}"] = np.asarray(inputs[f"tbl_{f}"])
    return {n: np.ascontiguousarray(v) for n, v in arrays.items()}


def kernel(**inputs):
    import concourse.bacc as _bacc
    from concourse.bass_utils import run_bass_kernel_spmd as _run

    nc = _bacc.Bacc("TRN2", target_bir_lowering=False, num_devices=1)
    arrays = _layout(inputs)
    aps = {n: nc.dram_tensor(f"in_{n}", v.shape, mybir.dt.from_np(v.dtype), kind="ExternalInput").ap()
           for n, v in arrays.items()}
    y = nc.dram_tensor("y_out", (BATCH, 1), F32, kind="ExternalOutput").ap()
    program(nc, aps, y)
    r = _run(nc, [{f"in_{n}": v for n, v in arrays.items()}], core_ids=[0])
    return r.results[0]["y_out"]
```

```python
from contextlib import ExitStack

import concourse.bass as bass
from concourse import mybir

F32 = mybir.dt.float32
F32R = mybir.dt.float32r
I32 = mybir.dt.int32
ALU = mybir.AluOpType
ACT = mybir.ActivationFunctionType
AX = mybir.AxisListType

P = 128
BATCH, F, D, H = 1024, 39, 16, 128
TB = P // D
TILES = P // TB
GT = 4
GROUPS = TILES // GT
BLOCKS = BATCH // P
SHIFTS = 21
SPC = 3
CH = SHIFTS // SPC
SPLIT = 3
HALVES = ((0, SPLIT), (SPLIT, CH))
KC = SPC * F
XW = F + SHIFTS - 1
FP = F + 1
UT = 2
UC = UT * P
UNITS = TILES // UT
JB = 4
FILLS = -(-F // JB)
YB = 5
DVE_FILLS = ((1, 4, 7), (1, 3, 6, 8))
ACT_FILLS = tuple(tuple(i for i in range(FILLS) if i not in d) for d in DVE_FILLS)
NADD = 11
PART = 2 * NADD
BIAS = F + 1
SLOTS = F + 2
L1D, L2D = 512, 256
HALF = 512
CIN1_FILLS = (4, 6, 8, 10, 12, 13, 15)
Z_FILL = 4
ROWS_FILLS = (1, 3, 5, 7)
GATHER_TILES = 11


def slot(j):
    return j if j < PART else j + 1


def view(base, dims):
    return bass.AP(tensor=base.tensor, offset=base.offset, ap=[list(base.ap[0])] + dims)


T_ROWS = TILES - GT
TR_BLOCK = GROUPS + 4


def tr_rows(q):
    return T_ROWS // GT + q


def tr_x0(t):
    return t // GT + (4 if t >= T_ROWS else 0)


def tr(B, n):
    return B * TR_BLOCK + (n + 1 + TR_BLOCK - tr_rows(0))


def tr_before(B, n):
    return B * TR_BLOCK + (n + TR_BLOCK - tr_rows(0))


def last_x0(B, t):
    g = t // GT
    return tr(B, tr_x0(GT * (g - 1))) if g else tr(B - 1, tr_x0(T_ROWS))


def unit(B, n):
    return B * UNITS + (n + 1)


def half_unit(B, n, half):
    return B * (2 * UNITS) + (2 * n + half + 1)


LOADS = 4


def loaded_by(B, n):
    return B * (UNITS // 2 * 16 * LOADS) + (n // 2 + 1) * 16 * LOADS


def tile(B, t):
    return B * TILES + (t + 2)


def done(B, t):
    return B * TILES + (t + 4)


def fill(B, t, i):
    return B * (TILES * FILLS) + (t * FILLS + i + 1)


def used(B, t, fills, i):
    even, odd = fills
    ahead = t // 2 * len(even + odd) + t % 2 * len(even) + len(odd)
    return B * (TILES // 2 * len(even + odd)) + (ahead + sum(f <= i for f in fills[t % 2]))


def program(nc, a, out):
    x0_dram = nc.dram_tensor("x0_rows", (2, XW, P * D), F32).ap()

    with ExitStack() as ctx:
        def sb(name, shape, dt=F32):
            return ctx.enter_context(nc.sbuf_tensor(name, shape, dt))

        def psum(name, shape):
            return ctx.enter_context(nc.psum_tensor(name, shape, F32))

        def sem(name):
            return ctx.enter_context(nc.semaphore(name))

        ident = sb("ident", [P, P])
        mask = sb("mask", [P, TB])
        w0 = sb("w0", [KC, CH, H])
        w0hi = sb("w0hi", [KC, CH - SPLIT, H], F32R)
        w0lo = sb("w0lo", [KC, CH - SPLIT, H], F32R)
        w1hi = sb("w1hi", [P, F * H], F32R)
        w1lo = sb("w1lo", [P, F * H], F32R)
        w2 = sb("w2", [P, F, H])
        wt1 = sb("wt1", [P, 3, L1D])
        wt1d = sb("wt1d", [D, L1D])
        wt2 = sb("wt2", [P, L1D // P, L2D])
        wt3 = sb("wt3", [P, L2D // P])
        biases = sb("biases", [P, 2])
        biases_d = sb("biases_d", [P, 2])
        bt1 = sb("bt1", [P, L1D // P])
        bt2 = sb("bt2", [P, L2D // P])
        ids = sb("ids", [P, BLOCKS + 1, F], I32)
        ids_now = sb("ids_now", [P, F], I32)
        rows = sb("rows", [P, F, D])
        x0t = sb("x0t", [P, P, D])
        x0 = sb("x0", [P, 2, GT, FP])
        xa = sb("xa", [KC, 2, UC])
        xb = sb("xb", [KC, 2, CH, UC])
        xh = sb("xh", [KC, CH - SPLIT, UC], F32R)
        xl = sb("xl", [KC, CH - SPLIT, UC], F32R)
        x1hi = sb("x1hi", [P, 2, UC], F32R)
        x1lo = sb("x1lo", [P, 2, UC], F32R)
        prod = sb("prod", [P, 2, SLOTS, H])
        x2 = sb("x2", [P, 2, H])
        diag = sb("diag", [P, 2, TB, FP])
        G = sb("G", [P, FP, P])
        z1 = sb("z1", [P, BATCH + 2 * TB])
        z2 = sb("z2", [P, BATCH + P])
        z3 = sb("z3", [P, BATCH + P])
        dense = sb("dense", [D, BATCH])
        w1raw = prod[:, 0, 0:F, :].rearrange("p j h -> p (j h)")
        w0b = xb[:, 1, :, 0:H]
        h1 = prod[:, 0, 0:L1D // P * BATCH // H, :].rearrange("p (m a) h -> p m (a h)", m=L1D // P)
        h2 = prod[:, 1, 0:L2D // P * BATCH // H, :].rearrange("p (m a) h -> p m (a h)", m=L2D // P)
        yrow = x0t[0:1, 0:BATCH // D, :].rearrange("p b d -> p (b d)")

        Y = psum("Y", [P, YB, 512])
        TR = psum("TR", [P, 512])
        X1P = psum("X1P", [P, 512])
        GZ = psum("GZ", [P, 512])
        GP = GZ[:, 0:TB * FP]
        ZP = GZ[:, 384:512]

        def rows_bank(B, q):
            return Y[:, q, :] if isinstance(B, int) else TR

        ids_in = sem("ids_in")
        consts_in = sem("consts_in")
        w0_in = sem("w0_in")
        w1_in = sem("w1_in")
        rest_in = sem("rest_in")
        stored = sem("stored")
        gathered = sem("gathered")
        ids_copied = sem("ids_copied")
        w0_ready = sem("w0_ready")
        w1hi_ready = sem("w1hi_ready")
        w1lo_ready = sem("w1lo_ready")
        bias_ready = sem("bias_ready")
        ones_ready = sem("ones_ready")
        x0t_zeroed = sem("x0t_zeroed")
        G_zeroed = sem("G_zeroed")
        x0_stored = sem("x0_stored")
        loaded = [sem("loaded_even"), sem("loaded_odd")]
        tr_full = sem("tr_full")
        tr_copied = sem("tr_copied")
        pairs_ready = sem("pairs_ready")
        pairs_high = sem("pairs_high")
        pairs_low = sem("pairs_low")
        x1_full = sem("x1_full")
        x1hi_ready = sem("x1hi_ready")
        x1lo_ready = sem("x1lo_ready")
        y_full = sem("y_full")
        y_act = sem("y_act")
        y_dve = sem("y_dve")
        added = sem("added")
        part_ready = sem("part_ready")
        x2_ready = sem("x2_ready")
        diag_ready = sem("diag_ready")
        g_full = sem("g_full")
        g_copied = sem("g_copied")
        z2_copied = sem("z2_copied")
        z3_full = sem("z3_full")
        z3_copied = sem("z3_copied")
        z1_done = sem("z1_done")
        h1_full = sem("h1_full")
        h1_ready = sem("h1_ready")
        h2_full = sem("h2_full")
        h2_ready = sem("h2_ready")
        y_row_full = sem("y_row_full")
        y_row = sem("y_row")

        block = ctx.enter_context(nc.Block())

        @block.sync
        def _(sp):
            def store_rows(B, copy):
                sp.wait_ge(tr_copied, tr(B, tr_rows(3)))
                rows_f = x0t[0:F, :, :].rearrange("f b d -> f (b d)")
                sp.dma_start(x0_dram[copy, 0:F, :], rows_f).then_inc(x0_stored, 16)
                sp.dma_start(x0_dram[copy, F:XW, :], rows_f[0:XW - F, :]).then_inc(x0_stored, 16)

            def load_unit(B, n, copy):
                if n == UNITS:
                    sp.wait_ge(x0_stored, B * 32 + 64)
                elif isinstance(B, int) and n == UNITS + 1:
                    sp.wait_ge(w0_ready, 3)
                else:
                    sp.wait_ge(x1_full, unit(B, n - 2))
                start = copy * XW * P * D + UC * (n % UNITS)
                for s in range(SPC):
                    src = bass.AP(tensor=x0_dram.tensor, offset=start + s * P * D,
                                  ap=[[P * D, F], [SPC * P * D, CH], [1, UC]])
                    sp.dma_start(xb[F * s:F * s + F, n % 2, :, :], src).then_inc(loaded[n % 2], 16)
                src = bass.AP(tensor=x0_dram.tensor, offset=start, ap=[[0, SPC], [P * D, F], [1, UC]])
                sp.dma_start(xa[:, n % 2, :], src).then_inc(loaded[n % 2], 16)

            sp.dma_start(ids[:, :, :], a["ids"]).then_inc(ids_in, 16)
            sp.dma_start(w1raw, a["w1"]).then_inc(w1_in, 16)
            sp.dma_start(ident[:, :], a["ident"]).then_inc(consts_in, 16)
            sp.dma_start(mask[:, :], a["mask"]).then_inc(consts_in, 16)
            sp.dma_start(biases[:, :], a["biases"]).then_inc(consts_in, 16)
            sp.dma_start(w0[:, :, :], a["w0a"]).then_inc(w0_in, 16)
            sp.dma_start(w0b, a["w0b"]).then_inc(w0_in, 16)
            for q in range(2):
                sp.dma_start(prod[:, q, BIAS, :], a["b1"].to_broadcast([P, H])).then_inc(rest_in, 16)
            sp.dma_start(w2[:, :, :], a["w2"]).then_inc(rest_in, 16)
            sp.dma_start(wt1[:, :, :], a["wt1"]).then_inc(rest_in, 16)
            sp.dma_start(wt1d[:, :], a["wt1d"]).then_inc(rest_in, 16)
            sp.dma_start(wt2[:, :, :], a["wt2"]).then_inc(rest_in, 16)
            sp.dma_start(wt3[:, :], a["wt3"]).then_inc(rest_in, 16)
            sp.dma_start(bt1[:, :], a["bt1"]).then_inc(rest_in, 16)
            sp.dma_start(bt2[:, :], a["bt2"]).then_inc(rest_in, 16)
            sp.dma_start(dense[:, :], a["dense"]).then_inc(rest_in, 16)
            store_rows(-1, 0)
            for n in range(UNITS, UNITS + 3):
                load_unit(-1, n, 0)
            with sp.Fori(0, BLOCKS, 2) as B0:
                for k in range(2):
                    for n in range(3, UNITS):
                        load_unit(B0 + k, n, k)
                    store_rows(B0 + k, 1 - k)
                    for n in range(UNITS, UNITS + 3):
                        load_unit(B0 + k, n, 1 - k)
            for q in range(2):
                sp.wait_ge(loaded[q], loaded_by(BLOCKS, 2 if q == 0 else 1))
            sp.wait_ge(y_row, 2)
            sp.dma_start(out.rearrange("b o -> o b"), yrow).then_inc(stored, 16)
            sp.wait_ge(stored, 16)

        REST = 10 * 16

        @block.gpsimd
        def _(pool):
            def gather(f):
                pool.indirect_dma_start(
                    out=rows[:, f, :], out_offset=None, in_=a[f"tbl_{f}"],
                    in_offset=bass.IndirectOffsetOnAxis(ap=ids_now[:, f:f + 1], axis=0),
                ).then_inc(gathered, 16)

            def next_ids(B):
                pool.tensor_copy(ids_now[:, :], ids[:, bass.ds(B + 1, 1), :].rearrange("p o f -> p (o f)")
                                 ).then_inc(ids_copied, 1)

            pool.wait_ge(ids_in, 16)
            pool.tensor_copy(ids_now[:, :], ids[:, 0, :]).then_inc(ids_copied, 1)
            pool.wait_ge(ids_copied, 1)
            for f in range(F):
                gather(f)
            pool.memset(x0[:, :, :, F:FP], 1.0).then_inc(ones_ready, 1)
            pool.memset(prod[:, 1, 0:BIAS, :], 0.0).then_inc(added, 1)
            pool.memset(G[:, :, :], 0.0).then_inc(G_zeroed, 1)
            pool.memset(diag[:, :, :, :], 0.0).then_inc(diag_ready, 3)
            pool.memset(x2[:, :, :], 0.0).then_inc(x2_ready, 2)
            pool.wait_ge(consts_in, 48)
            pool.wait_ge(ones_ready, 1)
            with pool.Fori(0, BLOCKS) as B:
                for t in range(TILES):
                    g, u, q = t // GT, t % GT, t % 2
                    if u == 0:
                        pool.wait_ge(tr_copied, last_x0(B, t))
                    pool.wait_ge(g_full, done(B, t - 2))
                    if t == 1:
                        pool.wait_ge(ids_copied, B + 2)
                    xs = x0[:, g % 2, u, :]
                    pool.tensor_tensor(diag[:, q, :, :], view(xs, [[0, TB], [1, FP]]),
                                       view(mask[:, :], [[1, TB], [0, FP]]), ALU.mult).then_inc(diag_ready, 1)
                    if t == 0:
                        pool.wait_ge(gathered, (B + 1) * (16 * F))
                        pool.wait_ge(tr_full, tr(B - 1, tr_rows(3)))
                        next_ids(B)
                    if 0 < t < GATHER_TILES:
                        for f in range(F * (t - 1) // (GATHER_TILES - 1), F * t // (GATHER_TILES - 1)):
                            gather(f)
                    pool.wait_ge(y_act, used(B, t, ACT_FILLS, (2 * NADD - 1) // JB))
                    pool.wait_ge(y_dve, used(B, t, DVE_FILLS, (2 * NADD - 1) // JB))
                    pool.tensor_tensor(prod[:, q, NADD:2 * NADD, :], prod[:, q, 0:NADD, :],
                                       prod[:, q, NADD:2 * NADD, :], ALU.add).then_inc(added, 1)
            pool.wait_ge(gathered, (BLOCKS + 1) * (16 * F))

        @block.tensor
        def _(pe):
            def rows_ready(B, q):
                if q == 0:
                    pe.wait_ge(gathered, (B + 2) * (16 * F))
                if not isinstance(B, int):
                    pe.wait_ge(tr_copied, tr_before(B, tr_rows(q)))

            def turn_rows(B, q):
                for e in range(4):
                    mm = pe.transpose(rows_bank(B, q)[0:F, P * e:P * e + P], rows[:, :, 4 * q + e], ident[:, :])
                mm.then_inc(tr_full, 1)

            def turn_x0(B, t):
                n = tr_x0(t)
                pe.wait_ge(tr_copied, tr_before(B, n))
                lo = (t + GT) % TILES
                for u in range(GT):
                    mm = pe.transpose(TR[:, P * u:P * u + P],
                                      x0t[:, (lo + u) * TB:(lo + u + 1) * TB, :].rearrange("f b d -> f (b d)"),
                                      ident[:, :])
                mm.then_inc(tr_full, 1)

            def cin1(B, n, c):
                if c == 0:
                    if not isinstance(B, int):
                        pe.wait_ge(x1lo_ready, half_unit(B, n - 1, 1))
                    pe.wait_ge(pairs_ready, half_unit(B, n, 0))
                x1p = X1P[:, 0:UC]
                k = c - SPLIT
                if k < 0:
                    pe.matmul(x1p, w0[:, c, :], xb[:, n % 2, c, :], start=(c == 0), stop=False)
                    return
                if k == 0:
                    pe.wait_ge(pairs_low, unit(B, n))
                pe.matmul(x1p, w0hi[:, k, :], xh[:, k, :], start=False, stop=False)
                pe.matmul(x1p, w0lo[:, k, :], xh[:, k, :], start=False, stop=False)
                mm = pe.matmul(x1p, w0hi[:, k, :], xl[:, k, :], start=False, stop=(c == CH - 1))
                if c == CH - 1:
                    mm.then_inc(x1_full, 1)

            def cin2(B, t, i):
                if i == 0 and t % UT == 0:
                    pe.wait_ge(x1hi_ready, unit(B, t // UT))
                    pe.wait_ge(x1lo_ready, half_unit(B, t // UT, 0))
                tb, ib = (t, i - YB) if i >= YB else (t - 1, i - YB + FILLS)
                if ib in ACT_FILLS[tb % 2]:
                    pe.wait_ge(y_act, used(B, tb, ACT_FILLS, ib))
                else:
                    pe.wait_ge(y_dve, used(B, tb, DVE_FILLS, ib))
                lo, hi = JB * H * i, min(JB * H * (i + 1), F * H)
                y = Y[:, (t * FILLS + i) % YB, 0:hi - lo]
                cols = slice(P * (t % UT), P * (t % UT) + P)
                x_hi = x1hi[:, t // UT % 2, cols]
                x_lo = x1lo[:, t // UT % 2, cols]
                pe.matmul(y, x_hi, w1hi[:, lo:hi], start=True, stop=False)
                pe.matmul(y, x_hi, w1lo[:, lo:hi], start=False, stop=False)
                if t == T_ROWS and i in ROWS_FILLS:
                    rows_ready(B, ROWS_FILLS.index(i))
                pe.matmul(y, x_lo, w1hi[:, lo:hi], start=False, stop=True).then_inc(y_full, 1)

            def cin3_g(B, t):
                pe.wait_ge(x2_ready, done(B, t))
                pe.wait_ge(diag_ready, done(B, t))
                pe.wait_ge(g_copied, done(B, t - 1))
                pe.matmul(GP, x2[:, t % 2, :], diag[:, t % 2, :, :].rearrange("p b j -> p (b j)"),
                          start=True, stop=True).then_inc(g_full, 1)

            def cin3_z(B, j):
                if j == 0:
                    pe.wait_ge(g_copied, done(B, -1))
                mm = pe.matmul(ZP, w2[:, j, :], G[:, j, :], start=(j == 0), stop=(j == F - 1))
                if j == F - 1:
                    mm.then_inc(z3_full, 1)

            pe.wait_ge(consts_in, 48)
            for q in range(4):
                rows_ready(-1, q)
                turn_rows(-1, q)
            turn_x0(-1, T_ROWS)
            pe.wait_ge(w0_ready, 3)
            for c in range(CH):
                cin1(-1, UNITS, c)
            pe.wait_ge(w1hi_ready, 1)
            pe.wait_ge(w1lo_ready, 1)
            pe.wait_ge(rest_in, REST)
            pe.wait_ge(G_zeroed, 1)
            pe.sem_inc(g_copied, 1)
            with pe.Fori(0, BLOCKS) as B:
                for t in range(TILES):
                    for i in range(FILLS):
                        cin2(B, t, i)
                        if t == T_ROWS and i in ROWS_FILLS:
                            turn_rows(B, ROWS_FILLS.index(i))
                        if t % GT == 0 and i == (9 if t == T_ROWS else 6):
                            turn_x0(B, t)
                        if i + FILLS * (t % UT) in CIN1_FILLS:
                            cin1(B, t // UT + 1, CIN1_FILLS.index(i + FILLS * (t % UT)))
                        if i == 1:
                            if t == 2:
                                pe.wait_ge(z3_copied, B + 1)
                            cin3_g(B, t - 2)
                        if t == 1 and i >= Z_FILL:
                            for j in range(F * (i - Z_FILL) // (FILLS - Z_FILL),
                                           F * (i + 1 - Z_FILL) // (FILLS - Z_FILL)):
                                cin3_z(B, j)

            def layer1(n):
                s = HALF * n
                parts = ((wt1d, dense[:, s:s + HALF]), (wt1[:, 1, :], z2[:, P + s:P + s + HALF]),
                         (wt1[:, 0, :], z1[:, s:s + HALF]), (wt1[:, 2, :], z3[:, P + s:P + s + HALF]))
                for m in range(L1D // P):
                    if n:
                        pe.wait_ge(h1_ready, L1D // P * (n - 1) + m + 1)
                    for k in range(3):
                        w, x = parts[k]
                        if k == 2 and n == 0 and m == 0:
                            pe.wait_ge(z1_done, 1)
                        pe.matmul(Y[:, m, :], w[:, P * m:P * m + P], x, start=(k == 0), stop=False)
                pe.wait_ge(z3_copied, HALF // P * (n + 1) + 1)
                for m in range(L1D // P):
                    w, x = parts[3]
                    pe.matmul(Y[:, m, :], w[:, P * m:P * m + P], x, start=False, stop=True).then_inc(h1_full, 1)

            def layer2(n):
                pe.wait_ge(h1_ready, L1D // P * (n + 1))
                for m in range(L2D // P):
                    if n:
                        pe.wait_ge(h2_ready, m + 1)
                    for k in range(L1D // P):
                        mm = pe.matmul([TR, Y[:, YB - 1, :]][m][:, :], wt2[:, k, P * m:P * m + P],
                                       h1[:, k, HALF * n:HALF * (n + 1)],
                                       start=(k == 0), stop=(k == L1D // P - 1))
                    mm.then_inc(h2_full, 1)

            def layer3(n):
                pe.wait_ge(h2_ready, L2D // P * (n + 1))
                for k in range(L2D // P):
                    mm = pe.matmul([X1P, GZ][n][0:1, :], wt3[:, k:k + 1], h2[:, k, HALF * n:HALF * (n + 1)],
                                   start=(k == 0), stop=(k == L2D // P - 1))
                mm.then_inc(y_row_full, 1)

            cin3_g(BLOCKS, -2)
            pe.wait_ge(y_act, used(BLOCKS, -1, ACT_FILLS, FILLS))
            pe.wait_ge(y_dve, used(BLOCKS, -1, DVE_FILLS, FILLS))
            pe.wait_ge(z2_copied, HALF // P + 1)
            layer1(0)
            cin3_g(BLOCKS, -1)
            layer2(0)
            for j in range(F):
                cin3_z(BLOCKS, j)
            pe.wait_ge(z2_copied, BLOCKS + 1)
            layer1(1)
            layer3(0)
            layer2(1)
            layer3(1)

        @block.scalar
        def _(act):
            def rows_out(B, q):
                n = tr_rows(q)
                act.wait_ge(tr_full, tr(B, n))
                act.activation(x0t[0:F, :, 4 * q:4 * q + 4].rearrange("f b e -> f e b"),
                               rows_bank(B, q)[0:F, :].rearrange("f (e b) -> f e b", e=4),
                               ACT.Copy).then_inc(tr_copied, 1)

            def x0_out(B, t):
                n = tr_x0(t)
                act.wait_ge(tr_full, tr(B, n))
                if not isinstance(B, int):
                    act.wait_ge(diag_ready, done(B, t - 1))
                    act.wait_ge(y_dve, used(B, t - 1, DVE_FILLS, FILLS))
                src = TR[:, :].rearrange("p (u f) -> p u f", u=GT)[:, :, 0:F]
                dst = x0[:, (t // GT + 1) % 2, :, :]
                act.activation(dst[:, :, 0:F], src, ACT.Copy).then_inc(tr_copied, 1)

            def high_part(B, n):
                act.wait_ge(pairs_ready, half_unit(B, n, 1))
                act.activation(xh[:, :, :], xb[:, n % 2, SPLIT:CH, :], ACT.Copy).then_inc(pairs_high, 1)

            def x1_out(B, n):
                act.wait_ge(x1_full, unit(B, n))
                act.activation(x1hi[:, n % 2, :], X1P[:, 0:UC], ACT.Identity,
                               bias=biases[:, 0:1]).then_inc(x1hi_ready, 1)

            def multiply(B, t, i):
                g, u = t // GT, t % GT
                act.wait_ge(y_full, fill(B, t, i))
                for j in range(JB * i, min(JB * (i + 1), F)):
                    k = j - JB * i
                    ins = act.activation(prod[:, t % 2, slot(j), :], Y[:, (t * FILLS + i) % YB, H * k:H * k + H],
                                         ACT.Copy, scale=x0[:, g % 2, u, j:j + 1])
                ins.then_inc(y_act, 1)

            def g_out(B, t):
                act.wait_ge(g_full, done(B, t))
                b = t % TILES * TB
                act.activation(G[:, :, b:b + TB].rearrange("k j b -> k b j"),
                               GP.rearrange("k (b j) -> k b j", b=TB), ACT.Copy).then_inc(g_copied, 1)

            def z2_out(B):
                act.wait_ge(g_copied, done(B, -1))
                act.activation(z2[:, bass.ds(B * P, P)], G[:, F, :], ACT.Copy).then_inc(z2_copied, 1)

            def z3_out(B):
                act.wait_ge(z3_full, B + 1)
                act.activation(z3[:, bass.ds(B * P, P)], ZP, ACT.Identity,
                               bias=biases_d[:, 1:2]).then_inc(z3_copied, 1)

            act.wait_ge(w1_in, 16)
            act.activation(w1hi[:, :], w1raw, ACT.Copy).then_inc(w1hi_ready, 1)
            act.wait_ge(consts_in, 48)
            act.activation(biases_d[:, :], biases[:, :], ACT.Copy, scale=float(D)).then_inc(bias_ready, 1)
            act.wait_ge(bias_ready, 1)
            act.wait_ge(x0t_zeroed, 1)
            for q in range(4):
                rows_out(-1, q)
            x0_out(-1, T_ROWS)
            high_part(-1, UNITS)
            x1_out(-1, UNITS)
            act.wait_ge(w1lo_ready, 1)
            act.wait_ge(G_zeroed, 1)
            act.sem_inc(y_act, len(ACT_FILLS[1]))
            act.sem_inc(g_full, 1)
            with act.Fori(0, BLOCKS) as B:
                for t in range(TILES):
                    if t % GT == 0:
                        act.wait_ge(tr_copied, last_x0(B, t))
                    act.wait_ge(x2_ready, done(B, t - 2))
                    if t == 2:
                        z3_out(B)
                    for i in range(FILLS):
                        if i in ACT_FILLS[t % 2]:
                            multiply(B, t, i)
                        if t == T_ROWS:
                            if i == ROWS_FILLS[0]:
                                act.wait_ge(x0_stored, (B + 1) * 32)
                            if i in ROWS_FILLS:
                                rows_out(B, ROWS_FILLS.index(i))
                        if i == 1:
                            g_out(B, t - 2)
                            if t == 1:
                                z2_out(B)
                        if t % UT == 0 and i == 3:
                            high_part(B, t // UT + 1)
                        if t % UT == 1 and i == 4:
                            x1_out(B, t // UT + 1)
                        if t % GT == 0 and i == (9 if t == T_ROWS else 6):
                            x0_out(B, t)

            def h1_out(n):
                for m in range(L1D // P):
                    act.wait_ge(h1_full, L1D // P * n + m + 1)
                    act.activation(h1[:, m, HALF * n:HALF * (n + 1)], Y[:, m, :], ACT.Relu,
                                   bias=bt1[:, m:m + 1]).then_inc(h1_ready, 1)

            def h2_out(n):
                for m in range(L2D // P):
                    act.wait_ge(h2_full, L2D // P * n + m + 1)
                    act.activation(h2[:, m, HALF * n:HALF * (n + 1)], [TR, Y[:, YB - 1, :]][m][:, :], ACT.Relu,
                                   bias=bt2[:, m:m + 1]).then_inc(h2_ready, 1)

            def y_out(n):
                act.wait_ge(y_row_full, n + 1)
                act.activation(yrow[:, HALF * n:HALF * (n + 1)], [X1P, GZ][n][0:1, :],
                               ACT.Copy).then_inc(y_row, 1)

            act.wait_ge(x1lo_ready, half_unit(BLOCKS, 0, 1))
            act.activation(z1[:, 0:BATCH], z1[:, 0:BATCH], ACT.Identity, bias=biases_d[:, 0:1]).then_inc(z1_done, 1)
            g_out(BLOCKS, -2)
            act.wait_ge(x2_ready, done(BLOCKS, -2))
            act.wait_ge(rest_in, REST)
            h1_out(0)
            g_out(BLOCKS, -1)
            z2_out(BLOCKS)
            act.wait_ge(x2_ready, done(BLOCKS, -1))
            h2_out(0)
            z3_out(BLOCKS)
            h1_out(1)
            y_out(0)
            h2_out(1)
            y_out(1)

        @block.vector
        def _(dve):
            def make_pairs(B, n, half):
                if half == 0:
                    dve.wait_ge(loaded[n % 2], loaded_by(B, n))
                lo, hi = HALVES[half]
                dve.tensor_tensor(xb[:, n % 2, lo:hi, :], xb[:, n % 2, lo:hi, :],
                                  view(xa[:, n % 2, :], [[0, hi - lo], [1, UC]]), ALU.mult).then_inc(pairs_ready, 1)

            def low_part(B, n):
                dve.wait_ge(pairs_high, unit(B, n))
                dve.tensor_tensor(xl[:, :, :], xb[:, n % 2, SPLIT:CH, :], xh[:, :, :].bitcast(F32),
                                  ALU.subtract).then_inc(pairs_low, 1)

            def x1_low(B, n):
                dve.wait_ge(x1hi_ready, unit(B, n))
                dve.scalar_tensor_tensor(out=x1lo[:, n % 2, :], in0=X1P[:, 0:UC], scalar=biases[:, 0:1],
                                         in1=x1hi[:, n % 2, :].bitcast(F32), op0=ALU.add,
                                         op1=ALU.subtract).then_inc(x1lo_ready, 1)

            def z1_sum(B, n):
                dve.tensor_reduce(z1[:, bass.ds(B * P + UT * TB * n, UT * TB)],
                                  X1P[:, 0:UC].rearrange("p (b d) -> p b d", d=D), AX.X, ALU.add
                                  ).then_inc(x1lo_ready, 1)

            def multiply(B, t, i):
                g, u = t // GT, t % GT
                dve.wait_ge(y_full, fill(B, t, i))
                xs = x0[:, g % 2, u, JB * i:JB * i + JB]
                dve.tensor_tensor(prod[:, t % 2, slot(JB * i):slot(JB * i) + JB, :],
                                  Y[:, (t * FILLS + i) % YB, :].rearrange("p (j h) -> p j h", h=H),
                                  view(xs, [[1, JB], [0, H]]), ALU.mult).then_inc(y_dve, 1)

            def add_up(dst, q, lo, hi, ready):
                dve.tensor_reduce(dst, prod[:, q, lo:hi, :].rearrange("p j h -> p h j"), AX.X, ALU.add
                                  ).then_inc(ready, 1)

            def part(B, t):
                dve.wait_ge(y_act, used(B, t, ACT_FILLS, FILLS))
                dve.wait_ge(y_dve, used(B, t, DVE_FILLS, FILLS))
                add_up(prod[:, t % 2, PART, :], t % 2, PART + 1, SLOTS, part_ready)

            def total(B, t):
                dve.wait_ge(part_ready, tile(B, t))
                dve.wait_ge(added, tile(B, t))
                dve.wait_ge(g_full, done(B, t - 2))
                add_up(x2[:, t % 2, :], t % 2, NADD, PART + 1, x2_ready)

            dve.memset(x0t[:, :, :], 0.0).then_inc(x0t_zeroed, 1)
            dve.wait_ge(w1_in, 16)
            dve.wait_ge(w1hi_ready, 1)
            dve.tensor_tensor(w1lo[:, :], w1raw, w1hi[:, :].bitcast(F32), ALU.subtract).then_inc(w1lo_ready, 1)
            dve.wait_ge(w0_in, 32)
            dve.tensor_tensor(w0[:, :, :], w0[:, :, :], w0b, ALU.add).then_inc(w0_ready, 1)
            dve.wait_ge(w0_ready, 1)
            dve.tensor_copy(w0hi[:, :, :], w0[:, SPLIT:CH, :]).then_inc(w0_ready, 1)
            dve.wait_ge(w0_ready, 2)
            dve.tensor_tensor(w0lo[:, :, :], w0[:, SPLIT:CH, :], w0hi[:, :, :].bitcast(F32),
                              ALU.subtract).then_inc(w0_ready, 1)
            for half in range(2):
                make_pairs(-1, UNITS, half)
            low_part(-1, UNITS)
            dve.wait_ge(consts_in, 48)
            x1_low(-1, UNITS)
            z1_sum(-1, UNITS)
            make_pairs(-1, UNITS + 1, 0)
            dve.wait_ge(rest_in, REST)
            dve.wait_ge(added, 1)
            dve.wait_ge(w1lo_ready, 1)
            dve.sem_inc(y_dve, len(DVE_FILLS[1]))
            with dve.Fori(0, BLOCKS) as B:
                for t in range(TILES):
                    for i in DVE_FILLS[t % 2]:
                        if i == 6:
                            x1_low(B, t // UT + 1)
                        multiply(B, t, i)
                        if i == 1:
                            if t % UT == 0:
                                make_pairs(B, t // UT + 1, 1)
                            part(B, t - 1)
                        if i == 4:
                            low_part(B, t // UT + 1)
                        if i in (3, 4):
                            total(B, t - 1)
                        if i == 6:
                            z1_sum(B, t // UT + 1)
                        if i == 8:
                            make_pairs(B, t // UT + 2, 0)
            part(BLOCKS, -1)
            total(BLOCKS, -1)


def _layout(inputs):
    import numpy as np

    ids = np.asarray(inputs["ids"])
    blocks = ids.reshape(BLOCKS, P, F).transpose(1, 0, 2)
    w0 = np.asarray(inputs["L0_rec_W0"]).reshape(H, F, F)
    w0a = np.zeros((SHIFTS, F, H), w0.dtype)
    w0b = np.zeros((SHIFTS, F, H), w0.dtype)
    j = np.arange(F)
    for s in range(SHIFTS - 1):
        k = (j + s) % F
        w0a[s] = w0[:, j, k].T
        if s:
            w0b[s] = w0[:, k, j].T

    def chunks(w):
        return w.reshape(CH, KC, H).transpose(1, 0, 2)

    wt1 = np.asarray(inputs["W_top1"])
    arrays = {
        "ids": np.concatenate([blocks, blocks[:, :1]], axis=1),
        "ident": np.eye(P, dtype=np.float32),
        "mask": np.repeat(np.eye(TB, dtype=np.float32), D, axis=0),
        "biases": np.stack([inputs["L0_rec_b0"], inputs["L0_rec_b2"]], axis=1),
        "b1": np.asarray(inputs["L0_rec_b1"]).reshape(1, H),
        "w0a": chunks(w0a),
        "w0b": chunks(w0b),
        "w1": np.asarray(inputs["L0_rec_W1"]).reshape(H, F, H).transpose(2, 1, 0).reshape(P, F * H),
        "w2": np.asarray(inputs["L0_rec_W2"]).reshape(H, F, H).transpose(2, 1, 0),
        "wt1": wt1[:3 * P].reshape(3, P, L1D).transpose(1, 0, 2),
        "wt1d": wt1[3 * P:],
        "wt2": np.asarray(inputs["W_top2"]).reshape(L1D // P, P, L2D).transpose(1, 0, 2),
        "wt3": np.asarray(inputs["W_top3"]).reshape(L2D // P, P).T,
        "bt1": np.asarray(inputs["b_top1"]).reshape(L1D // P, P).T,
        "bt2": np.asarray(inputs["b_top2"]).reshape(L2D // P, P).T,
        "dense": np.asarray(inputs["dense_ctx"]).T,
    }
    for f in range(F):
        arrays[f"tbl_{f}"] = np.asarray(inputs[f"tbl_{f}"])
    return {n: np.ascontiguousarray(v) for n, v in arrays.items()}


def kernel(**inputs):
    import concourse.bacc as _bacc
    from concourse.bass_utils import run_bass_kernel_spmd as _run

    nc = _bacc.Bacc("TRN2", target_bir_lowering=False, num_devices=1)
    arrays = _layout(inputs)
    aps = {n: nc.dram_tensor(f"in_{n}", v.shape, mybir.dt.from_np(v.dtype), kind="ExternalInput").ap()
           for n, v in arrays.items()}
    y = nc.dram_tensor("y_out", (BATCH, 1), F32, kind="ExternalOutput").ap()
    program(nc, aps, y)
    r = _run(nc, [{f"in_{n}": v for n, v in arrays.items()}], core_ids=[0])
    return r.results[0]["y_out"]
```
